# Optimizing a Trainium2 kernel written in Bass

```python
import numpy as np
import jax
import jax.numpy as jnp

def _softmax(x, axis=-1):
    return jax.nn.softmax(x, axis=axis)

def _gelu(x):
    return jax.nn.gelu(x, approximate=True)

def _silu(x):
    return jax.nn.silu(x)

def _sigmoid(x):
    return jax.nn.sigmoid(x)

def _layernorm(x, axis=-1, eps=1e-05):
    m = jnp.mean(x, axis=axis, keepdims=True)
    v = jnp.var(x, axis=axis, keepdims=True)
    return (x - m) / jnp.sqrt(v + eps)

def _scatter_add(tgt, idx, src, axis=0):
    return tgt.at[idx].add(src)

def _segment_sum(src, seg, n):
    return jax.ops.segment_sum(src, seg, n)
kernel_name = 'mk_prb_d1_jaxref_r8_ebe768'

def setup_inputs(seed: int=0):
    np.random.seed(seed)
    _w = jnp.asarray

    def _L0_attn_setup():
        import jax, jax.numpy as jnp
        import numpy as np
        NUM_HEADS = 16
        HIDDEN = 128
        HEAD_DIM = HIDDEN // NUM_HEADS

        def _rope_cos_sin(S, head_dim):
            inv = 1.0 / 10000.0 ** (jnp.arange(0, head_dim, 2, dtype=jnp.float32) / head_dim)
            t = jnp.arange(S, dtype=jnp.float32)
            ang = jnp.outer(t, inv)
            return (jnp.cos(ang), jnp.sin(ang))

        def _apply_rope(x, cos, sin):
            B, S, nh, hd = x.shape
            xr = x[..., 0::2]
            xi = x[..., 1::2]
            c = cos[None, :, None, :]
            s = sin[None, :, None, :]
            or_ = xr * c - xi * s
            oi_ = xr * s + xi * c
            return jnp.stack([or_, oi_], axis=-1).reshape(B, S, nh, hd)
        key = jax.random.key(seed)
        k1, k2, k3, k4, k5 = jax.random.split(key, 5)
        std = 1.0 / np.sqrt(HIDDEN)
        return {'x': jax.random.normal(k1, (2, 256, HIDDEN), dtype=jnp.float32), 'wq': jax.random.normal(k2, (HIDDEN, HIDDEN), dtype=jnp.float32) * std, 'wk': jax.random.normal(k3, (HIDDEN, HIDDEN), dtype=jnp.float32) * std, 'wv': jax.random.normal(k4, (HIDDEN, HIDDEN), dtype=jnp.float32) * std, 'wo': jax.random.normal(k5, (HIDDEN, HIDDEN), dtype=jnp.float32) * std}
    _L0_attn_in = _L0_attn_setup()

    def _L0_ffn_setup():
        import jax, jax.numpy as jnp
        import numpy as np
        DIM = 128
        MOE_HID = 64
        SHARED_HID = 256
        N_EXPERTS = 16
        TOP_K = 2
        NORM_TOPK_PROB = True
        key = jax.random.key(seed)
        ks = jax.random.split(key, 9)
        s = 0.02
        x = jax.random.normal(ks[0], (2, 128, DIM), dtype=jnp.float32)
        Wg = jax.random.normal(ks[1], (N_EXPERTS, DIM), dtype=jnp.float32) * s
        We_gate = jax.random.normal(ks[2], (N_EXPERTS, MOE_HID, DIM), dtype=jnp.float32) * s
        We_up = jax.random.normal(ks[3], (N_EXPERTS, MOE_HID, DIM), dtype=jnp.float32) * s
        We_down = jax.random.normal(ks[4], (N_EXPERTS, DIM, MOE_HID), dtype=jnp.float32) * s
        Ws_gate = jax.random.normal(ks[5], (SHARED_HID, DIM), dtype=jnp.float32) * s
        Ws_up = jax.random.normal(ks[6], (SHARED_HID, DIM), dtype=jnp.float32) * s
        Ws_down = jax.random.normal(ks[7], (DIM, SHARED_HID), dtype=jnp.float32) * s
        Wsg = jax.random.normal(ks[8], (1, DIM), dtype=jnp.float32) * s
        return {'x': x, 'Wg': Wg, 'We_gate': We_gate, 'We_up': We_up, 'We_down': We_down, 'Ws_gate': Ws_gate, 'Ws_up': Ws_up, 'Ws_down': Ws_down, 'Wsg': Wsg}
    _L0_ffn_in = _L0_ffn_setup()
    _d = {'L0_attn_x': _L0_attn_in['x'], 'L0_attn_wq': _L0_attn_in['wq'], 'L0_attn_wk': _L0_attn_in['wk'], 'L0_attn_wv': _L0_attn_in['wv'], 'L0_attn_wo': _L0_attn_in['wo'], 'L0_ffn_Wg': _L0_ffn_in['Wg'], 'L0_ffn_We_gate': _L0_ffn_in['We_gate'], 'L0_ffn_We_up': _L0_ffn_in['We_up'], 'L0_ffn_We_down': _L0_ffn_in['We_down'], 'L0_ffn_Ws_gate': _L0_ffn_in['Ws_gate'], 'L0_ffn_Ws_up': _L0_ffn_in['Ws_up'], 'L0_ffn_Ws_down': _L0_ffn_in['Ws_down'], 'L0_ffn_Wsg': _L0_ffn_in['Wsg']}
    _x0 = _d['L0_attn_x']
    _d['L0_attn_x'] = jax.random.normal(jax.random.fold_in(jax.random.key(seed), 1), (32, 256, 128), dtype=_x0.dtype)
    del _x0
    return _d

def reference(L0_attn_x, L0_attn_wq, L0_attn_wk, L0_attn_wv, L0_attn_wo, L0_ffn_Wg, L0_ffn_We_gate, L0_ffn_We_up, L0_ffn_We_down, L0_ffn_Ws_gate, L0_ffn_Ws_up, L0_ffn_Ws_down, L0_ffn_Wsg):

    def _L0_attn_ref(x, wq, wk, wv, wo):
        import jax, jax.numpy as jnp
        import numpy as np
        NUM_HEADS = 16
        HIDDEN = 128
        HEAD_DIM = HIDDEN // NUM_HEADS

        def _rope_cos_sin(S, head_dim):
            inv = 1.0 / 10000.0 ** (jnp.arange(0, head_dim, 2, dtype=jnp.float32) / head_dim)
            t = jnp.arange(S, dtype=jnp.float32)
            ang = jnp.outer(t, inv)
            return (jnp.cos(ang), jnp.sin(ang))

        def _apply_rope(x, cos, sin):
            B, S, nh, hd = x.shape
            xr = x[..., 0::2]
            xi = x[..., 1::2]
            c = cos[None, :, None, :]
            s = sin[None, :, None, :]
            or_ = xr * c - xi * s
            oi_ = xr * s + xi * c
            return jnp.stack([or_, oi_], axis=-1).reshape(B, S, nh, hd)
        B, S, H = x.shape
        nh, hd = (NUM_HEADS, HEAD_DIM)
        xq = jnp.einsum('bsh,oh->bso', x, wq).reshape(B, S, nh, hd)
        xk = jnp.einsum('bsh,oh->bso', x, wk).reshape(B, S, nh, hd)
        xv = jnp.einsum('bsh,oh->bso', x, wv).reshape(B, S, nh, hd)
        cos, sin = _rope_cos_sin(S, hd)
        xq = _apply_rope(xq.astype(jnp.float32), cos, sin).astype(x.dtype)
        xk = _apply_rope(xk.astype(jnp.float32), cos, sin).astype(x.dtype)
        scores = jnp.einsum('bqhd,bkhd->bhqk', xq, xk) / np.sqrt(hd)
        probs = jax.nn.softmax(scores.astype(jnp.float32), axis=-1).astype(xq.dtype)
        out = jnp.einsum('bhqk,bkhd->bqhd', probs, xv).reshape(B, S, nh * hd)
        return jnp.einsum('bso,ho->bsh', out, wo)

    def _L0_ffn_ref(x, Wg, We_gate, We_up, We_down, Ws_gate, Ws_up, Ws_down, Wsg):
        import jax, jax.numpy as jnp
        import numpy as np
        DIM = 128
        MOE_HID = 64
        SHARED_HID = 256
        N_EXPERTS = 16
        TOP_K = 2
        NORM_TOPK_PROB = True
        B, S, D = x.shape
        xt = x.reshape(-1, D)
        gates = jax.nn.softmax(xt @ Wg.T, axis=-1)
        scores, inds = jax.lax.top_k(gates, TOP_K)
        if NORM_TOPK_PROB:
            scores = scores / jnp.sum(scores, axis=-1, keepdims=True)
        g = jnp.einsum('td,ehd->teh', xt, We_gate)
        u = jnp.einsum('td,ehd->teh', xt, We_up)
        h = jax.nn.silu(g) * u
        y_all = jnp.einsum('teh,edh->ted', h, We_down)
        y_sel = jnp.take_along_axis(y_all, inds[:, :, None], axis=1)
        y = jnp.sum(y_sel * scores[:, :, None], axis=1)
        shared = jax.nn.silu(xt @ Ws_gate.T) * (xt @ Ws_up.T) @ Ws_down.T
        y = y + jax.nn.sigmoid(xt @ Wsg.T) * shared
        return y.reshape(B, S, D)
    x = L0_attn_x
    xn = _layernorm(x, axis=-1)
    x = x + _L0_attn_ref(xn, L0_attn_wq, L0_attn_wk, L0_attn_wv, L0_attn_wo) + _L0_ffn_ref(xn, L0_ffn_Wg, L0_ffn_We_gate, L0_ffn_We_up, L0_ffn_We_down, L0_ffn_Ws_gate, L0_ffn_Ws_up, L0_ffn_Ws_down, L0_ffn_Wsg)
    return x

_drawn_inputs = setup_inputs


def setup_inputs(seed=0):
    import zlib

    import numpy as np

    out = dict(_drawn_inputs(seed))
    spreads = {}
    factors = {'L0_ffn_Wg': 8.0,
     'L0_ffn_We_gate': 8.0,
     'L0_ffn_We_up': 8.0,
     'L0_ffn_We_down': 8.0,
     'L0_ffn_Ws_gate': 8.0,
     'L0_ffn_Ws_up': 8.0,
     'L0_ffn_Ws_down': 8.0,
     'L0_ffn_Wsg': 8.0}
    for name, (base, spread) in spreads.items():
        noise = np.random.default_rng([zlib.crc32(name.encode()), seed]).standard_normal(out[name].shape)
        drawn = base * np.exp(spread * noise) if base else spread * noise
        out[name] = jnp.asarray(drawn.astype(out[name].dtype))
    for name, factor in factors.items():
        out[name] = (out[name] * factor).astype(out[name].dtype)
    return out
```

```python
from contextlib import ExitStack

import numpy as np

import concourse.bass as bass
from concourse import mybir

F32 = mybir.dt.float32
BF16 = mybir.dt.bfloat16
U32 = mybir.dt.uint32
ALU = mybir.AluOpType
ACT = mybir.ActivationFunctionType
AX_X = mybir.AxisListType.X

P = 128
B, S, D = 32, 256, 128
T = S // P
H, HD = 16, 8
E, EH = 16, 64
SH = 256
PAIRS = E * EH // P
CHUNKS = PAIRS + SH // P
VG = D + E + 1
GATES = E + 1
QUADS = H // 4
HPAD = 32
SCALE = float(1.0 / np.sqrt(HD))
EPS = 1e-5

Q_PARTS = (0, 1, 2, 0, 1, 0)
K_PARTS = (0, 0, 0, 1, 1, 2)
PARTS = 3
SLOT_ROWS = 96
SHIFT_ROWS = 2

COLS = {}
_at = 0
for _name, _n in (("ident", P), ("wqk", 4 * D), ("wvg", VG), ("iota", E), ("cos", S), ("sin", S),
                  ("wo", D), ("wgu", CHUNKS * 2 * P), ("wd", CHUNKS * D)):
    COLS[_name] = (_at, _at + _n)
    _at += _n
CONST_COLS = _at
FIRST_COLS = COLS["sin"][1]

PREP, SCAN, MAIN, TAIL = "PREP", "SCAN", "MAIN", "TAIL"
RUNS_IN = {PREP: (-2, B - 3), SCAN: (-1, B - 2), MAIN: (0, B - 1), TAIL: (1, B)}
FULL = (1, B - 3)
LOOP_FROM = 2
DEPTH = 3

V_ORDER = ([("s0", SCAN), ("s1", SCAN), ("max1", MAIN), ("s2", SCAN), ("s3", SCAN), ("out0", TAIL),
            ("out1", TAIL), ("s4", SCAN), ("s5", SCAN), ("rope0", PREP), ("s6", SCAN), ("rope1", PREP),
            ("s7", SCAN), ("vg", PREP), ("s8", SCAN), ("s9", SCAN), ("s10", SCAN), ("max0", SCAN)]
           + [(f"s{h}", SCAN) for h in range(11, H)] + [("gates", PREP)])
A_ORDER = ([(f"e{h}", MAIN) for h in range(5)] + [("xnT", PREP)] + [("e5", MAIN), ("e6", MAIN), ("outT", TAIL)]
           + [(f"e{h}", MAIN) for h in range(7, H)])


def has(stage, it):
    return RUNS_IN[stage][0] <= it <= RUNS_IN[stage][1]


def is_at(it, n):
    return isinstance(it, int) and it == n


class Ring:

    def __init__(self, order):
        self.order = order
        self.full = len(order)
        self.before_full = self._before(FULL[0])

    def _before(self, it):
        return sum(sum(has(stage, j) for _, stage in self.order) for j in range(-2, it))

    def before(self, it):
        if isinstance(it, int) and not FULL[0] <= it <= FULL[1] + 1:
            return self._before(it)
        return (it - FULL[0]) * self.full + self.before_full

    def index(self, name, stages):
        return [n for n, stage in self.order if stage in stages].index(name)

    def fill(self, name, it, stages):
        return self.before(it) + self.index(name, stages)

    def bank(self, name, stages, static_before):
        return (static_before + self.index(name, stages)) % 2

    def behind(self, name, it):
        if isinstance(it, int):
            before = [n for n, stage in self.order if has(stage, it - 1)]
            return self._before(it - 1) + before.index(name) + 1 if name in before else 0
        return self.before(it) - self.full + [n for n, _ in self.order].index(name) + 1


def due(count):
    return not isinstance(count, int) or count > 0


def build(nc, x, consts, out):
    with ExitStack() as ctx:
        def sb(name, shape, dt=F32):
            return ctx.enter_context(nc.sbuf_tensor(name, shape, dt))

        def bank(name):
            return ctx.enter_context(nc.psum_tensor(name, [P, 512], F32))

        def sem(name):
            return ctx.enter_context(nc.semaphore(name))

        parts_dram = nc.dram_tensor("parts_dram", (DEPTH, P, 2, PARTS, S), BF16, kind="Internal").ap()
        shift_dram = nc.dram_tensor("shift_dram", (DEPTH, 2, H // 2 * T, SHIFT_ROWS, P), BF16, kind="Internal").ap()
        gates_dram = nc.dram_tensor("gates_dram", (DEPTH, GATES, S), F32, kind="Internal").ap()

        const = sb("const", [P, CONST_COLS])

        def c(name):
            return const[:, COLS[name][0]:COLS[name][1]]

        ident, wo = c("ident"), c("wo")
        wqk = c("wqk").rearrange("p (m o) -> p m o", m=4)
        wgu = c("wgu").rearrange("p (c g o) -> p c g o", c=CHUNKS, g=2)
        wd = c("wd").rearrange("p (c o) -> p c o", c=CHUNKS)
        cos, sin = c("cos"), c("sin")

        xin = sb("xin", [P, DEPTH, T, D])
        xres = sb("xres", [P, DEPTH, T, D])
        xnT = sb("xnT", [P, DEPTH, S])
        qrows = [sb(f"qrows{i}", [P, H, S], BF16) for i in range(DEPTH)]
        krows = [sb(f"krows{i}", [P, H, S], BF16) for i in range(DEPTH)]
        values = sb("values", [P, DEPTH, T, H, HPAD])
        gates_b = [sb(f"gates_b{i}", [P, PAIRS + 1, S]) for i in range(DEPTH)]
        stats = sb("stats", [P, T, 6])
        moments = sb("moments", [P, T, 2])
        var_eps = sb("var_eps", [P, T])
        minus_half = sb("minus_half", [P, T])
        rstd = sb("rstd", [P, T])
        xn = sb("xn", [P, T, D])
        logits = sb("logits", [P, T, GATES])
        top = sb("top", [P, T, 8])
        top_at = sb("top_at", [P, T, 8], U32)
        top_atf = sb("top_atf", [P, T, 2])
        gap = sb("gap", [P, T, 2])
        gap_exp = sb("gap_exp", [P, T, 2])
        gap_one = sb("gap_one", [P, T, 2])
        gap_rec = sb("gap_rec", [P, T, 2])
        first_w = sb("first_w", [P, T, 2])
        second_w = sb("second_w", [P, T, 1])
        pick_a = sb("pick_a", [P, T, E])
        pick_b = sb("pick_b", [P, T, E])
        gates = sb("gates", [P, T, GATES])
        gates_t = sb("gates_t", [32, S])
        rope_c = sb("rope_c", [P, 2, S])
        rope_s = sb("rope_s", [P, 2, S])
        qk = sb("qk", [P, 2, S])
        qk_rest = sb("qk_rest", [P, 2, S])
        parts = sb("parts", [P, 2, PARTS, S], BF16)
        row_max = sb("row_max", [P, 2, H // 2 * T])
        shift = sb("shift", [H // 2 * T, 2, SHIFT_ROWS, P], BF16)
        PB = 4
        probs = sb("probs", [P, PB, T, S])
        heads_t = sb("heads_t", [P, QUADS, S])
        den_rec = sb("den_rec", [P, T, H])
        heads = sb("heads", [P, T, D])
        out_t = sb("out_t", [P, S])
        tanh = sb("tanh", [P, 2, S])
        act = sb("act", [P, 2, S])
        HU = 5
        hidden_u = sb("hidden_u", [P, HU, S])
        hidden = sb("hidden", [P, CHUNKS, S])
        result = sb("result", [P, DEPTH, T, D])

        v_bank = [bank(f"v_bank{i}") for i in range(2)]
        a_bank = [bank(f"a_bank{i}") for i in range(2)]
        gu_bank = [bank(f"gu_bank{i}") for i in range(2)]
        pv_bank = bank("pv_bank")
        y_bank = bank("y_bank")

        consts_loaded = sem("consts_loaded")
        consts2_loaded = sem("consts2_loaded")
        ones_set = sem("ones_set")
        x_loaded = sem("x_loaded")
        xres_loaded = sem("xres_loaded")
        stats_done = sem("stats_done")
        moments_done = sem("moments_done")
        var_eps_done = sem("var_eps_done")
        rstd_done = sem("rstd_done")
        xn_done = sem("xn_done")
        v_filled, v_free = sem("v_filled"), sem("v_free")
        a_filled, a_free = sem("a_filled"), sem("a_free")
        gu_filled = sem("gu_filled")
        tanh_done = sem("tanh_done")
        act_done = sem("act_done")
        hidden_u_done = sem("hidden_u_done")
        hidden_done = sem("hidden_done")
        down_done = sem("down_done")
        pv_done = sem("pv_done")
        heads_t_done = sem("heads_t_done")
        den_done = sem("den_done")
        y_done = sem("y_done")
        result_done = sem("result_done")
        stored = sem("stored")
        rope_cos_done = sem("rope_cos_done")
        split_step = sem("split_step")
        parts_done = sem("parts_done")
        parts_stored = sem("parts_stored")
        rows_loaded = sem("rows_loaded")
        shift_hi_done = sem("shift_hi_done")
        shift_done = sem("shift_done")
        shift_stored = sem("shift_stored")
        shift_loaded = sem("shift_loaded")
        top_done = sem("top_done")
        top_at_done = sem("top_at_done")
        picks_done = sem("picks_done")
        gap_done = sem("gap_done")
        gap_exp_done = sem("gap_exp_done")
        gap_step = sem("gap_step")
        gates_done = sem("gates_done")
        gates_t_done = sem("gates_t_done")
        gates_stored = sem("gates_stored")
        gates_loaded = sem("gates_loaded")

        V, A = Ring(V_ORDER), Ring(A_ORDER)
        SPLIT = 4
        READS = 2 * len(Q_PARTS)

        def iterations(eng, iteration):
            def one(it):
                iteration(it, it % DEPTH, [s for s in (PREP, SCAN, MAIN, TAIL) if has(s, it)])
            for it in range(-2, LOOP_FROM):
                one(it)
            trips = (FULL[1] - LOOP_FROM + 1) // DEPTH
            end = LOOP_FROM + trips * DEPTH
            with eng.Fori(LOOP_FROM, end - DEPTH + 1, DEPTH) as i:
                for j in range(DEPTH):
                    iteration(i + j if j else i, (LOOP_FROM + j) % DEPTH, [PREP, SCAN, MAIN, TAIL])
            for it in range(end, B + 1):
                one(it)

        def static_before(ring, it, stages):
            return ring.before(it) if isinstance(it, int) else ring.before_full

        assert V.full % 2 == 0 and A.full % 2 == 0

        block = ctx.enter_context(nc.Block())

        @block.tensor
        def _(pe):
            mm = nc.tensor.matmul

            def iteration(it, phase, stages):
                prep, scan, main, tail = (s in stages for s in (PREP, SCAN, MAIN, TAIL))
                bp, bs, bm, bt = (phase + 2) % DEPTH, (phase + 1) % DEPTH, phase, (phase - 1) % DEPTH

                def v_fill(name):
                    n = V.fill(name, it, stages)
                    if due(n - 1):
                        pe.wait_ge(v_free, n - 1)
                    return v_bank[V.bank(name, stages, static_before(V, it, stages))]

                def a_fill(name):
                    n = A.fill(name, it, stages)
                    if due(n - 1):
                        pe.wait_ge(a_free, n - 1)
                    return a_bank[A.bank(name, stages, static_before(A, it, stages))]

                def weighted_values(h, of, buf, seq):
                    quad, j = h // 4, h % 4
                    if h % 8 == 0:
                        if due(2 * seq + h // 8):
                            pe.wait_ge(heads_t_done, 2 * seq + h // 8)
                    if of == "now":
                        pe.wait_ge(a_free, A.fill(f"e{h}", it, stages) + 1)
                    else:
                        pe.wait_ge(a_free, A.behind(f"e{h}", it))
                    for t in range(T):
                        last = mm(pv_bank[32 * j:32 * j + 32, quad % 2 * S:quad % 2 * S + S],
                                  values[:, buf, t, h, :], probs[:, h % PB, t, :],
                                  start=(t == 0), stop=(t == T - 1))
                    last.then_inc(pv_done, 1)

                for s in range(H):
                    if main:
                        if s == 0:
                            pe.wait_ge(shift_loaded, 16 * (2 * it + 1))
                        if s == H // 2:
                            pe.wait_ge(shift_loaded, 16 * (2 * it + 2))
                        dst = a_fill(f"e{s}")
                        n = SLOT_ROWS + SHIFT_ROWS
                        for t in range(T):
                            last = mm(dst[:, t * S:(t + 1) * S], krows[bm][0:n, s, t * P:(t + 1) * P],
                                      qrows[bm][0:n, s, :], start=True, stop=True)
                        last.then_inc(a_filled, 1)
                    if scan:
                        if s == 0:
                            pe.wait_ge(rows_loaded, 16 * READS * (it + 2))
                        dst = v_fill(f"s{s}")
                        for t in range(T):
                            last = mm(dst[:, t * S:(t + 1) * S], qrows[bs][0:SLOT_ROWS, s, t * P:(t + 1) * P],
                                      krows[bs][0:SLOT_ROWS, s, :], start=True, stop=True)
                        last.then_inc(v_filled, 1)
                    if tail and s < 2:
                        weighted_values(H - 2 + s, "before", bt, it - 1)
                    if main and s >= 2:
                        weighted_values(s - 2, "now", bm, it)
                    if main and s < CHUNKS:
                        if due(CHUNKS * it + s - 1):
                            pe.wait_ge(hidden_u_done, CHUNKS * it + s - 1)
                        if is_at(it, 0) and s == 0:
                            pe.wait_ge(consts2_loaded, 16)
                        for g in range(2):
                            last = mm(gu_bank[s % 2][:, g * S:(g + 1) * S], wgu[:, s, g, :], xnT[:, bm, :],
                                      start=True, stop=True)
                        last.then_inc(gu_filled, 1)
                    if main and s >= 9:
                        for ch in [x for x in (2 * (s - 9), 2 * (s - 9) + 1) if x < CHUNKS]:
                            if ch == 0:
                                if due(it):
                                    pe.wait_ge(result_done, it)
                            pe.wait_ge(hidden_done, CHUNKS * it + ch + 1)
                            for t in range(T):
                                last = mm(y_bank[:, t * D:(t + 1) * D], hidden[:, ch, t * P:(t + 1) * P],
                                          wd[:, ch, :], start=(ch == 0 and t == 0), stop=False,
                                          skip_group_check=True)
                            last.then_inc(down_done, 1)

                    if main and s == 1:
                        pe.wait_ge(v_free, V.behind(f"s{H - 1}", it))
                        dst = v_fill("max1")
                        nc.tensor.transpose(dst[0:H // 2 * T, 0:P], row_max[:, 1, :],
                                            ident).then_inc(v_filled, 1)
                    if tail and s == 3:
                        pe.wait_ge(heads_t_done, 2 * it)
                        for t in range(T):
                            dst = v_fill(f"out{t}")
                            for quad in range(QUADS):
                                last = nc.tensor.transpose(dst[:, quad * P:(quad + 1) * P],
                                                           heads_t[:, quad, t * P:(t + 1) * P], ident)
                            last.then_inc(v_filled, 1)
                    if prep and s == 4:
                        pe.wait_ge(xn_done, T * (it + 3))
                        if is_at(it, -2):
                            pe.wait_ge(consts_loaded, 16)
                        dst = a_fill("xnT")
                        for t in range(T):
                            last = nc.tensor.transpose(dst[:, t * P:(t + 1) * P], xn[:, t, :], ident)
                        last.then_inc(a_filled, 1)
                    if prep and s in (5, 6):
                        if s == 5:
                            pe.wait_ge(a_free, A.fill("xnT", it, stages) + 1)
                        dst = v_fill(f"rope{s - 5}")
                        for m in range(2):
                            last = mm(dst[:, m * S:(m + 1) * S], wqk[:, 2 * m + s - 5, :], xnT[:, bp, :],
                                      start=True, stop=True)
                        last.then_inc(v_filled, 1)
                    if tail and s == 6:
                        pe.wait_ge(v_free, V.fill("out1", it, stages) + 1)
                        dst = a_fill("outT")
                        for t in range(T):
                            last = nc.tensor.transpose(dst[:, t * P:(t + 1) * P], heads[:, t, :], ident)
                        last.then_inc(a_filled, 1)
                    if prep and s == 7:
                        dst = v_fill("vg")
                        for t in range(T):
                            last = mm(dst[:, t * VG:(t + 1) * VG], xnT[:, bp, t * P:(t + 1) * P], c("wvg"),
                                      start=True, stop=True)
                        last.then_inc(v_filled, 1)
                    if tail and s == 8:
                        pe.wait_ge(a_free, A.fill("outT", it, stages) + 1)
                        for t in range(T):
                            last = mm(y_bank[:, t * D:(t + 1) * D], out_t[:, t * P:(t + 1) * P], wo,
                                      start=False, stop=(t == T - 1), skip_group_check=True)
                        last.then_inc(y_done, 1)
                    if scan and s == 10:
                        pe.wait_ge(v_free, V.fill("s7", it, stages) + 1)
                        dst = v_fill("max0")
                        nc.tensor.transpose(dst[0:H // 2 * T, 0:P], row_max[:, 0, :], ident).then_inc(v_filled, 1)
                    if prep and s == H - 1:
                        pe.wait_ge(gates_done, it + 3)
                        dst = v_fill("gates")
                        for t in range(T):
                            last = nc.tensor.transpose(dst[0:GATES, t * P:(t + 1) * P], gates[:, t, :], ident)
                        last.then_inc(v_filled, 1)

            iterations(pe, iteration)

        @block.scalar
        def _(act_e):
            act_fn = nc.scalar.activation

            def iteration(it, phase, stages):
                prep, scan, main, tail = (s in stages for s in (PREP, SCAN, MAIN, TAIL))
                bp = (phase + 2) % DEPTH

                def filled(name):
                    act_e.wait_ge(a_filled, A.fill(name, it, stages) + 1)
                    return a_bank[A.bank(name, stages, static_before(A, it, stages))]

                def copy_heads(half, n, seq):
                    act_e.wait_ge(pv_done, H * seq + 8 * (half + 1))
                    act_fn(heads_t[:, 2 * half:2 * half + 2, :],
                           pv_bank[:, :].rearrange("p (q s) -> p q s", q=2), ACT.Copy).then_inc(heads_t_done, 1)

                for s in range(H):
                    if main:
                        src = filled(f"e{s}")
                        if due(H * it + s - PB + 1):
                            act_e.wait_ge(pv_done, H * it + s - PB + 1)
                        act_fn(probs[:, s % PB, :, :], src[:, :].rearrange("p (t s) -> p t s", t=T), ACT.Exp,
                               scale=SCALE).then_inc(a_free, 1)
                    if main and s < CHUNKS:
                        act_e.wait_ge(gu_filled, CHUNKS * it + s + 1)
                        if due(CHUNKS * it + s - 1):
                            act_e.wait_ge(act_done, CHUNKS * it + s - 1)
                        act_fn(tanh[:, s % 2, :], gu_bank[s % 2][:, 0:S], ACT.Tanh, scale=0.5).then_inc(tanh_done, 1)
                    if tail and s == 1:
                        copy_heads(1, s, it - 1)
                    if main and s == 10:
                        copy_heads(0, s, it)
                    if prep and s == 4:
                        src = filled("xnT")
                        act_fn(xnT[:, bp, :], src[:, 0:S], ACT.Copy).then_inc(a_free, 1)
                    if tail and s == 6:
                        src = filled("outT")
                        act_fn(out_t[:, :], src[:, 0:S], ACT.Copy).then_inc(a_free, 1)
                    if prep and s == 13:
                        act_e.wait_ge(gap_done, 2 * (it + 3))
                        act_fn(gap_exp[:, :, :], gap[:, :, :], ACT.Exp).then_inc(gap_exp_done, 1)

            iterations(act_e, iteration)

        @block.vector
        def _(dve):
            v = nc.vector
            v.memset(minus_half[:, :], -0.5).then_inc(ones_set, 1)
            for i in range(DEPTH):
                v.memset(qrows[i][:, :, :].bitcast(F32), 0.0).then_inc(ones_set, 1)
                v.memset(krows[i][0:SLOT_ROWS, :, :].bitcast(F32), 0.0).then_inc(ones_set, 1)
                v.memset(krows[i][SLOT_ROWS:P, :, :], 1.0).then_inc(ones_set, 1)
            v.memset(values[:, :, :, :, :], 0.0).then_inc(ones_set, 1)
            dve.wait_ge(ones_set, 3 * DEPTH + 2)
            v.memset(values[:, :, :, :, HD:HD + 1], 1.0).then_inc(ones_set, 1)
            dve.wait_ge(ones_set, 3 * DEPTH + 3)

            def iteration(it, phase, stages):
                prep, scan, main, tail = (s in stages for s in (PREP, SCAN, MAIN, TAIL))
                bp, bt = (phase + 2) % DEPTH, (phase - 1) % DEPTH
                sp = it + 2

                def filled(name):
                    dve.wait_ge(v_filled, V.fill(name, it, stages) + 1)
                    return v_bank[V.bank(name, stages, static_before(V, it, stages))]

                def shifts(half, n, seq):
                    src = filled(f"max{half}")
                    rows = H // 2 * T
                    if due(16 * (n - 1)):
                        dve.wait_ge(shift_stored, 16 * (n - 1))
                    v.tensor_scalar(shift[:, half, 0, :], src[0:rows, 0:P], -1.0, None, ALU.mult)\
                        .then_inc(shift_hi_done, 1)
                    dve.wait_ge(shift_hi_done, n + 1)
                    v.scalar_tensor_tensor(out=shift[:, half, 1, :], in0=src[0:rows, 0:P], scalar=-1.0,
                                           in1=shift[:, half, 0, :], op0=ALU.mult, op1=ALU.subtract)\
                        .then_inc(v_free, 1)

                for s in range(H):
                    if main and s < CHUNKS:
                        dve.wait_ge(tanh_done, CHUNKS * it + s + 1)
                        if due(CHUNKS * it + s - 1):
                            dve.wait_ge(hidden_u_done, CHUNKS * it + s - 1)
                        v.scalar_tensor_tensor(out=act[:, s % 2, :], in0=tanh[:, s % 2, :], scalar=1.0,
                                               in1=gu_bank[s % 2][:, 0:S], op0=ALU.add, op1=ALU.mult)\
                            .then_inc(act_done, 1)
                    if prep and s == 1:
                        dve.wait_ge(stats_done, T * (sp + 1))
                        if due(T * sp):
                            dve.wait_ge(xn_done, T * sp)
                    if prep and s == 9:
                        dve.wait_ge(v_free, V.fill("vg", it, stages) + 1)
                    if prep and s == 10:
                        dve.wait_ge(top_done, T * (sp + 1))
                    if scan:
                        src = filled(f"s{s}")
                        at = s % 8 * T
                        if s == 0 and due(V.behind("max0", it)):
                            dve.wait_ge(v_filled, V.behind("max0", it))
                        if s == 8 and main:
                            dve.wait_ge(v_filled, V.fill("max1", it, stages) + 1)
                        v.tensor_reduce(row_max[:, s // 8, at:at + T], src[:, :].rearrange("p (t k) -> p t k", t=T),
                                        AX_X, ALU.max).then_inc(v_free, 1)
                    if main and s < CHUNKS:
                        n = CHUNKS * it + s
                        dve.wait_ge(act_done, n + 1)
                        if due(n - HU + 1):
                            dve.wait_ge(hidden_done, n - HU + 1)
                        v.tensor_tensor(hidden_u[:, s % HU, :], act[:, s % 2, :],
                                        gu_bank[s % 2][:, S:2 * S], ALU.mult).then_inc(hidden_u_done, 1)

                    if prep and s == 0:
                        dve.wait_ge(x_loaded, 16 * (sp + 1))
                        if due(T * sp):
                            dve.wait_ge(moments_done, T * sp)
                        for t in range(T):
                            v.bn_stats(stats[:, t, :], xin[:, bp, t, :]).then_inc(stats_done, 1)
                    if prep and s == 1:
                        for t in range(T):
                            v.bn_aggr(moments[:, t, :], stats[:, t, :]).then_inc(moments_done, 1)
                    if main and s == 1:
                        shifts(1, 2 * it + 1, it)
                    if prep and s == 2:
                        dve.wait_ge(moments_done, T * (sp + 1))
                        if due(sp):
                            dve.wait_ge(rstd_done, sp)
                        v.tensor_scalar(var_eps[:, :], moments[:, :, 1], EPS, None, ALU.add).then_inc(var_eps_done, 1)
                    if prep and s == 3:
                        dve.wait_ge(rstd_done, sp + 1)
                        if due(A.behind("xnT", it)):
                            dve.wait_ge(a_filled, A.behind("xnT", it))
                        for t in range(T):
                            v.tensor_scalar(xn[:, t, :], xin[:, bp, t, :], moments[:, t, 0:1], rstd[:, t:t + 1],
                                            ALU.subtract, ALU.mult).then_inc(xn_done, 1)
                    if tail and s == 3:
                        for t in range(T):
                            src = filled(f"out{t}")[:, :].rearrange("p (h r) -> p h r", r=HPAD)
                            v.reciprocal(den_rec[:, t, :], src[:, :, HD]).then_inc(den_done, 1)
                            dve.wait_ge(den_done, T * (it - 1) + t + 1)
                            if t == 0:
                                if due(A.behind("outT", it)):
                                    dve.wait_ge(a_filled, A.behind("outT", it))
                            v.tensor_tensor(heads[:, t, :].rearrange("p (h d) -> p h d", d=HD), src[:, :, 0:HD],
                                            den_rec[:, t, :].unsqueeze(2).to_broadcast([P, H, HD]),
                                            ALU.mult).then_inc(v_free, 1)
                    if prep and s == 5:
                        if is_at(it, -2):
                            dve.wait_ge(consts_loaded, 16)
                        src = filled("rope0")[:, :].rearrange("p (m s) -> p m s", m=2)
                        if due(SPLIT * sp):
                            dve.wait_ge(split_step, SPLIT * sp)
                        v.tensor_tensor(rope_c[:, :, :], src, cos.unsqueeze(1).to_broadcast([P, 2, S]),
                                        ALU.mult).then_inc(v_free, 1)
                    if prep and s == 6:
                        src = filled("rope1")[:, :].rearrange("p (m s) -> p m s", m=2)
                        v.tensor_tensor(rope_s[:, :, :], src, sin.unsqueeze(1).to_broadcast([P, 2, S]),
                                        ALU.mult).then_inc(v_free, 1)
                    if prep and s == 7:
                        src = filled("vg")[:, 0:T * VG].rearrange("p (t c) -> p t c", t=T)
                        if due(sp):
                            dve.wait_ge(gates_done, sp)
                        for t in range(T):
                            v.tensor_copy(values[:, bp, t, :, 0:HD],
                                          src[:, t, 0:D].rearrange("p (h d) -> p h d", d=HD))
                        v.tensor_copy(logits[:, :, :], src[:, :, D:VG]).then_inc(v_free, 1)
                    if tail and s == 8:
                        dve.wait_ge(y_done, it)
                        dve.wait_ge(xres_loaded, 16 * it)
                        if due(16 * (it - 1)):
                            dve.wait_ge(stored, 16 * (it - 1))
                        v.tensor_tensor(result[:, bt, :, :], y_bank[:, 0:T * D].rearrange("p (t d) -> p t d", t=T),
                                        xres[:, bt, :, :], ALU.add).then_inc(result_done, 1)
                    if scan and s == 10:
                        shifts(0, 2 * (it + 1), it + 1)
                    if prep and s == 9:
                        for t in range(T):
                            v.max(top[:, t, :], logits[:, t, 0:E]).then_inc(top_done, 1)
                    if prep and s == 10:
                        for t in range(T):
                            v.max_index(top_at[:, t, :], top[:, t, :], logits[:, t, 0:E]).then_inc(top_at_done, 1)
                        v.tensor_tensor(gap[:, :, 0], top[:, :, 1], top[:, :, 0], ALU.subtract).then_inc(gap_done, 1)
                        v.tensor_scalar(gap[:, :, 1], logits[:, :, E], -1.0, None, ALU.mult).then_inc(gap_done, 1)
                    if prep and s == 12:
                        dve.wait_ge(top_at_done, T * (sp + 1))
                        v.tensor_copy(top_atf[:, :, :], top_at[:, :, 0:2]).then_inc(gap_step, 1)
                    if prep and s == 13:
                        dve.wait_ge(gap_exp_done, sp + 1)
                        v.tensor_scalar(gap_one[:, :, :], gap_exp[:, :, :], 1.0, None, ALU.add).then_inc(gap_step, 1)
                        dve.wait_ge(gap_step, 5 * sp + 2)
                        v.reciprocal(gap_rec[:, :, :], gap_one[:, :, :]).then_inc(gap_step, 1)
                        dve.wait_ge(gap_step, 5 * sp + 3)
                        v.tensor_scalar(first_w[:, :, :], gap_rec[:, :, :], 0.5, None, ALU.mult).then_inc(gap_step, 1)
                    if prep and s == 14:
                        dve.wait_ge(gap_step, 5 * sp + 4)
                        v.tensor_tensor(second_w[:, :, :], gap_exp[:, :, 0:1], first_w[:, :, 0:1], ALU.mult)\
                            .then_inc(gap_step, 1)
                        for t in range(T):
                            v.tensor_scalar(pick_a[:, t, :], c("iota"), top_atf[:, t, 0:1], first_w[:, t, 0:1],
                                            ALU.is_equal, ALU.mult).then_inc(picks_done, 1)
                        dve.wait_ge(gap_step, 5 * sp + 5)
                        for t in range(T):
                            v.tensor_scalar(pick_b[:, t, :], c("iota"), top_atf[:, t, 1:2], second_w[:, t, 0:1],
                                            ALU.is_equal, ALU.mult).then_inc(picks_done, 1)
                        if due(V.behind("gates", it)):
                            dve.wait_ge(v_filled, V.behind("gates", it))
                        v.tensor_copy(gates[:, :, E:GATES], first_w[:, :, 1:2]).then_inc(picks_done, 1)
                        dve.wait_ge(picks_done, 5 * (sp + 1))
                        v.tensor_tensor(gates[:, :, 0:E], pick_a[:, :, :], pick_b[:, :, :], ALU.add)\
                            .then_inc(gates_done, 1)
                    if prep and s == H - 1:
                        src = filled("gates")
                        if due(16 * sp):
                            dve.wait_ge(gates_stored, 16 * sp)
                        v.tensor_copy(gates_t[0:GATES, :], src[0:GATES, 0:S]).then_inc(v_free, 1)

            iterations(dve, iteration)

        @block.gpsimd
        def _(pool):
            g = nc.gpsimd

            def iteration(it, phase, stages):
                prep, scan, main, tail = (s in stages for s in (PREP, SCAN, MAIN, TAIL))
                sp = it + 2
                for s in range(H):
                    if scan and s == 6:
                        pool.wait_ge(gates_loaded, 16 * 3 * (it + 2))
                    if main and s < CHUNKS:
                        pool.wait_ge(hidden_u_done, CHUNKS * it + s + 1)
                        if due(CHUNKS * (it - 1) + s + 1):
                            pool.wait_ge(down_done, CHUNKS * (it - 1) + s + 1)
                        g.tensor_tensor(hidden[:, s, :], hidden_u[:, s % HU, :],
                                        gates_b[phase][:, min(s, PAIRS), :], ALU.mult).then_inc(hidden_done, 1)
                    if prep and s == 2:
                        if is_at(it, -2):
                            pool.wait_ge(ones_set, 1)
                        pool.wait_ge(var_eps_done, sp + 1)
                        if due(T * sp):
                            pool.wait_ge(xn_done, T * sp)
                        g.tensor_tensor(rstd[:, :], var_eps[:, :], minus_half[:, :], ALU.pow).then_inc(rstd_done, 1)
                    if prep and s == 6:
                        pool.wait_ge(v_free, V.fill("rope1", it, stages) + 1)
                        if due(sp):
                            pool.wait_ge(parts_done, sp)
                        g.tensor_tensor(qk[:, :, :], rope_c[:, :, :], rope_s[:, :, :], ALU.add).then_inc(split_step, 1)
                    if prep and s == 7:
                        if due(16 * sp):
                            pool.wait_ge(parts_stored, 16 * sp)
                        g.tensor_tensor(parts[:, :, 0, :], rope_c[:, :, :], rope_s[:, :, :], ALU.add)\
                            .then_inc(split_step, 1)
                    if prep and s == 8:
                        pool.wait_ge(split_step, SPLIT * sp + 2)
                        g.tensor_tensor(qk_rest[:, :, :], qk[:, :, :], parts[:, :, 0, :], ALU.subtract)\
                            .then_inc(split_step, 1)
                    if prep and s == 9:
                        g.tensor_tensor(parts[:, :, 1, :], qk[:, :, :], parts[:, :, 0, :], ALU.subtract)\
                            .then_inc(split_step, 1)
                    if prep and s == 10:
                        pool.wait_ge(split_step, SPLIT * sp + 4)
                        g.tensor_tensor(parts[:, :, 2, :], qk_rest[:, :, :], parts[:, :, 1, :], ALU.subtract)\
                            .then_inc(parts_done, 1)

            iterations(pool, iteration)

        @block.sync
        def _(sp_e):
            dma = sp_e.dma_start

            def rows_of(ap, seq):
                return ap[seq].rearrange("(p t) d -> p t d", t=T)

            dma(const[:, 0:FIRST_COLS], consts[:, 0:FIRST_COLS]).then_inc(consts_loaded, 16)
            dma(xin[:, 0, :, :], rows_of(x, 0)).then_inc(x_loaded, 16)
            dma(const[:, FIRST_COLS:], consts[:, FIRST_COLS:]).then_inc(consts2_loaded, 16)

            def iteration(it, phase, stages):
                prep, scan, main, tail = (s in stages for s in (PREP, SCAN, MAIN, TAIL))
                bp, bs, bm, bt = (phase + 2) % DEPTH, (phase + 1) % DEPTH, phase, (phase - 1) % DEPTH
                seq = it + 2

                def move_shifts(half, n, buf):
                    sp_e.wait_ge(v_free, V.fill(f"max{half}", it, stages) + 1)
                    dma(shift_dram[buf, half], shift[:, half, :, :]).then_inc(shift_stored, 16)
                    sp_e.wait_ge(shift_stored, 16 * (n + 1))
                    cols = slice(half * H // 2, (half + 1) * H // 2)
                    dma(qrows[buf][SLOT_ROWS:SLOT_ROWS + SHIFT_ROWS, cols, :].rearrange("r h (t q) -> r (h t) q", t=T),
                        shift_dram[buf, half].rearrange("c r q -> r c q")).then_inc(shift_loaded, 16)

                if main:
                    move_shifts(1, 2 * it + 1, bm)
                if prep and not is_at(it, RUNS_IN[PREP][1]):
                    sp_e.wait_ge(xn_done, T * (it + 3))
                    dma(xin[:, phase, :, :], rows_of(x, it + 3)).then_inc(x_loaded, 16)
                if tail:
                    sp_e.wait_ge(result_done, it)
                    dma(rows_of(out, it - 1), result[:, bt, :, :]).then_inc(stored, 16)
                if main:
                    dma(xres[:, bm, :, :], rows_of(x, it)).then_inc(xres_loaded, 16)
                if prep:
                    sp_e.wait_ge(parts_done, seq + 1)
                    dma(parts_dram[bp], parts[:, :, :, :]).then_inc(parts_stored, 16)
                    if is_at(it, -2):
                        sp_e.wait_ge(ones_set, 3 * DEPTH + 3)
                    sp_e.wait_ge(parts_stored, 16 * (seq + 1))
                    for rows, m, slots in ((qrows[bp], 0, Q_PARTS), (krows[bp], 1, K_PARTS)):
                        for slot, part in enumerate(slots):
                            dma(rows[HD * slot:HD * (slot + 1), :, :],
                                parts_dram[bp, :, m, part, :].rearrange("(h d) c -> d h c", d=HD))\
                                .then_inc(rows_loaded, 16)
                if scan:
                    move_shifts(0, 2 * (it + 1), bs)
                if prep:
                    sp_e.wait_ge(v_free, V.fill("gates", it, stages) + 1)
                    dma(gates_dram[bp], gates_t[0:GATES, :]).then_inc(gates_stored, 16)
                    sp_e.wait_ge(gates_stored, 16 * (seq + 1))
                    for half in range(2):
                        dma(gates_b[bp][half * EH:(half + 1) * EH, 0:PAIRS, :],
                            gates_dram[bp, half:E:2, :].partition_broadcast(EH)).then_inc(gates_loaded, 16)
                    dma(gates_b[bp][:, PAIRS, :], gates_dram[bp, E, :].partition_broadcast(P))\
                        .then_inc(gates_loaded, 16)

            iterations(sp_e, iteration)
            sp_e.wait_ge(stored, 16 * B)


def constants():
    token = (T * np.arange(P)[None, :] + np.arange(T)[:, None]).reshape(S).astype(np.float32)
    inv = (1.0 / 10000.0 ** (np.arange(0, HD, 2, dtype=np.float32) / HD)).astype(np.float32)
    angle = inv[:, None] * token[None, :]
    cos = np.tile(np.repeat(np.cos(angle), 2, axis=0), (H, 1))
    sin = np.tile(np.stack([-np.sin(angle), np.sin(angle)], axis=1).reshape(HD, S), (H, 1))
    return np.eye(P, dtype=np.float32), np.tile(np.arange(E, dtype=np.float32), (P, 1)), \
        cos.astype(np.float32), sin.astype(np.float32)


def kernel(L0_attn_x, L0_attn_wq, L0_attn_wk, L0_attn_wv, L0_attn_wo, L0_ffn_Wg, L0_ffn_We_gate, L0_ffn_We_up,
           L0_ffn_We_down, L0_ffn_Ws_gate, L0_ffn_Ws_up, L0_ffn_Ws_down, L0_ffn_Wsg):
    import concourse.bacc as bacc
    from concourse.bass_utils import run_bass_kernel_spmd

    ident, iota, cos, sin = constants()
    swap = np.arange(D).reshape(D // 2, 2)[:, ::-1].reshape(D)
    a = [np.asarray(w) for w in (L0_attn_wq, L0_attn_wk, L0_attn_wv, L0_attn_wo, L0_ffn_Wg, L0_ffn_Wsg)]
    wq, wk, wv, wo, wg, wsg = a
    eg, eu, ed, sg, su, sd = [np.asarray(w) for w in (L0_ffn_We_gate, L0_ffn_We_up, L0_ffn_We_down,
                                                      L0_ffn_Ws_gate, L0_ffn_Ws_up, L0_ffn_Ws_down)]
    gate = np.concatenate([eg.reshape(E * EH, D), sg]).reshape(CHUNKS, P, D)
    up = np.concatenate([eu.reshape(E * EH, D), su]).reshape(CHUNKS, P, D)
    gate_up = np.stack([gate, up], axis=1).transpose(3, 0, 1, 2).reshape(D, CHUNKS * 2 * P)
    down = np.concatenate([ed.transpose(0, 2, 1).reshape(E * EH, D), sd.T]).reshape(CHUNKS, P, D)
    down = down.transpose(1, 0, 2).reshape(P, CHUNKS * D)
    consts = np.concatenate([ident, wq.T, wq[swap].T, wk.T, wk[swap].T, wv.T, wg.T, wsg.T, iota, cos, sin,
                             wo.T, gate_up, down], axis=1)
    arrays = {"x": np.ascontiguousarray(L0_attn_x), "consts": np.ascontiguousarray(consts)}

    nc = bacc.Bacc("TRN2", target_bir_lowering=False, num_devices=1)
    x_ap = nc.dram_tensor("x", (B, S, D), F32, kind="ExternalInput").ap()
    c_ap = nc.dram_tensor("consts", (P, CONST_COLS), F32, kind="ExternalInput").ap()
    o_ap = nc.dram_tensor("out", (B, S, D), F32, kind="ExternalOutput").ap()
    build(nc, x_ap, c_ap, o_ap)
    r = run_bass_kernel_spmd(nc, [arrays], core_ids=[0])
    return r.results[0]["out"]
```

```python
from contextlib import ExitStack

import numpy as np

import concourse.bass as bass
from concourse import mybir

F32 = mybir.dt.float32
BF16 = mybir.dt.bfloat16
F32R = mybir.dt.float32r
U32 = mybir.dt.uint32
ALU = mybir.AluOpType
ACT = mybir.ActivationFunctionType
AX_X = mybir.AxisListType.X

P = 128
B, S, D = 32, 256, 128
T = S // P
H, HD = 16, 8
E, EH = 16, 64
SH = 256
PAIRS = E * EH // P
CHUNKS = PAIRS + SH // P
VG = D + E + 2
GATES = E + 1
QUADS = H // 4
HPAD = 32
SCALE = float(1.0 / np.sqrt(HD))
EPS = 1e-5
TWO_ONES = float(np.array([0x3F803F80], np.uint32).view(np.float32)[0])

SETS = (((2, 0), (1, 1), (0, 2)), ((1, 0), (0, 1), (0, 0)))
PARTS = 3
SET_ROWS = PARTS * HD
PART_AT = (slice(2, 4), slice(1, 5, 3), slice(0, 6, 5))
SLOT_ROWS = 96
SHIFT_ROWS = 2


COLS = {}
_at = 0
for _name, _n in (("ident", P), ("iota", E), ("cos", S), ("sin", S), ("wo", D), ("wd", CHUNKS * D),
                  ("wqk", 4 * D), ("wvg", VG), ("wgu", CHUNKS * 2 * P)):
    COLS[_name] = (_at, _at + _n)
    _at += _n
CONST_COLS = _at
SPLIT_FROM = COLS["wqk"][0]
SPLIT_COLS = CONST_COLS - SPLIT_FROM
SMALL_COLS = COLS["wgu"][0]

NORM, PREP, SCAN, MAIN, TAIL = "NORM", "PREP", "SCAN", "MAIN", "TAIL"
RUNS_IN = {NORM: (-3, B - 4), PREP: (-2, B - 3), SCAN: (-1, B - 2), MAIN: (0, B - 1), TAIL: (1, B)}
STAGES = (NORM, PREP, SCAN, MAIN, TAIL)
FIRST, LAST = -3, B
FULL = (1, B - 4)
LOOP_FROM = 2
DEPTH = 3

CHUNK_SLOT = [c * H // CHUNKS for c in range(CHUNKS)]
LAST_DOWN_SLOT = CHUNK_SLOT[-1] + 3 - H
CHUNK_IN = {s: c for c, s in enumerate(CHUNK_SLOT)}

V_EXTRA = {1: ("max1", (MAIN,)), 2: ("rope0", (PREP,)), 3: ("rope1", (PREP,)), 4: ("vg", (PREP,)),
           5: ("out0", (TAIL,)), 6: ("out1", (TAIL,)), 9: ("wo_max0", (TAIL, SCAN)), 11: ("gates", (PREP,))}
V_ORDER = [x for h in range(H) for x in [(f"s{h}", (SCAN,))] + ([V_EXTRA[h]] if h in V_EXTRA else [])]
A_EXTRA = {0: ("xnT", (PREP,)), 7: ("outT", (TAIL,))}
A_ORDER = [x for h in range(H) for x in [(f"e{h}", (MAIN,))] + ([A_EXTRA[h]] if h in A_EXTRA else [])]


def has(stages, it):
    return any(RUNS_IN[stage][0] <= it <= RUNS_IN[stage][1] for stage in stages)


def is_at(it, n):
    return isinstance(it, int) and it == n


class Ring:

    def __init__(self, order):
        self.order = order
        self.full = len(order)
        self.before_full = self._before(FULL[0])

    def _before(self, it):
        return sum(sum(has(of, j) for _, of in self.order) for j in range(FIRST, it))

    def before(self, it):
        if isinstance(it, int) and not FULL[0] <= it <= FULL[1] + 1:
            return self._before(it)
        return (it - FULL[0]) * self.full + self.before_full

    def index(self, name, stages):
        return [n for n, of in self.order if set(of) & set(stages)].index(name)

    def fill(self, name, it, stages):
        return self.before(it) + self.index(name, stages)

    def bank(self, name, stages, static_before):
        return (static_before + self.index(name, stages)) % 2

    def behind(self, name, it):
        if isinstance(it, int):
            before = [n for n, of in self.order if has(of, it - 1)]
            return self._before(it - 1) + before.index(name) + 1 if name in before else 0
        return self.before(it) - self.full + [n for n, _ in self.order].index(name) + 1


def due(count):
    return not isinstance(count, int) or count > 0


def build(nc, x, consts, out):
    with ExitStack() as ctx:
        def sb(name, shape, dt=F32):
            return ctx.enter_context(nc.sbuf_tensor(name, shape, dt))

        def bank(name):
            return ctx.enter_context(nc.psum_tensor(name, [P, 512], F32))

        def sem(name):
            return ctx.enter_context(nc.semaphore(name))

        parts_dram = nc.dram_tensor("parts_dram", (DEPTH, len(SETS), 2, P, PARTS, S), BF16, kind="Internal").ap()
        shift_dram = nc.dram_tensor("shift_dram", (DEPTH, 2, H // 2 * T, SHIFT_ROWS, P), BF16, kind="Internal").ap()
        gates_dram = nc.dram_tensor("gates_dram", (DEPTH, GATES, S), F32, kind="Internal").ap()

        const = sb("const", [P, CONST_COLS])

        def c(name):
            return const[:, COLS[name][0]:COLS[name][1]]

        ident, wo = c("ident"), c("wo")
        weights = [sb(f"weights_{part}", [P, SPLIT_COLS], F32R) for part in ("high", "low")]

        def split(name):
            return [w[:, COLS[name][0] - SPLIT_FROM:COLS[name][1] - SPLIT_FROM] for w in weights]

        wqk = [w.rearrange("p (m o) -> p m o", m=4) for w in split("wqk")]
        wvg = split("wvg")
        wgu = [w.rearrange("p (c g o) -> p c g o", c=CHUNKS, g=2) for w in split("wgu")]
        PASSES = ((0, 0), (0, 1), (1, 0))
        wd = c("wd").rearrange("p (c o) -> p c o", c=CHUNKS)
        cos, sin = c("cos"), c("sin")

        xin = sb("xin", [P, DEPTH, T, D])
        xres = sb("xres", [P, DEPTH, T, D])
        xnT_full = sb("xnT_full", [P, S])
        xnT = [sb(f"xnT_{part}", [P, DEPTH, S], F32R) for part in ("high", "low")]
        rows = [sb(f"rows{i}", [P, 2, H, S], BF16) for i in range(DEPTH)]
        qrows, krows = [r[:, 0] for r in rows], [r[:, 1] for r in rows]
        values = sb("values", [P, DEPTH, T, H, HPAD])
        gates_b = [sb(f"gates_b{i}", [P, PAIRS + 1, S]) for i in range(DEPTH)]
        stats = sb("stats", [P, T, 6])
        moments = sb("moments", [P, T, 2])
        var_eps = sb("var_eps", [P, T])
        minus_half = sb("minus_half", [P, T])
        rstd = sb("rstd", [P, T])
        xn = sb("xn", [P, T, D])
        logits = sb("logits", [P, T, GATES])
        top = sb("top", [P, T, 8])
        top_at = sb("top_at", [P, T, 8], U32)
        top_atf = sb("top_atf", [P, T, 2])
        gap = sb("gap", [P, T, 2])
        gap_exp = sb("gap_exp", [P, T, 2])
        gap_one = sb("gap_one", [P, T, 2])
        gap_rec = sb("gap_rec", [P, T, 2])
        first_w = sb("first_w", [P, T, 2])
        second_w = sb("second_w", [P, T, 1])
        pick_a = sb("pick_a", [P, T, E])
        pick_b = sb("pick_b", [P, T, E])
        gates = sb("gates", [P, T, GATES])
        gates_t = sb("gates_t", [32, S])
        rope_c = sb("rope_c", [P, 2, S])
        rope_s = sb("rope_s", [P, 2, S])
        qk = sb("qk", [P, 2, S])
        qk_rest = sb("qk_rest", [P, 2, S])
        parts = sb("parts", [P, 2 * PARTS, S], BF16)
        row_max = sb("row_max", [P, 2, H // 2 * T])
        shift = sb("shift", [H // 2 * T, 2, SHIFT_ROWS, P], BF16)
        PB = 4
        probs = sb("probs", [P, PB, T, S])
        heads_t = sb("heads_t", [P, QUADS, S])
        den_rec = sb("den_rec", [P, T, H])
        heads = sb("heads", [P, T, D])
        out_t = sb("out_t", [P, S])
        tanh = sb("tanh", [P, 2, S])
        act = sb("act", [P, 2, S])
        HU = 5
        hidden_u = sb("hidden_u", [P, HU, S])
        hidden = sb("hidden", [P, CHUNKS, S])
        partial = sb("partial", [P, T, D])
        result = sb("result", [P, T, D])

        v_bank = [bank(f"v_bank{i}") for i in range(2)]
        a_bank = [bank(f"a_bank{i}") for i in range(2)]
        gu_bank = [bank(f"gu_bank{i}") for i in range(2)]
        pv_bank = bank("pv_bank")
        y_bank = bank("y_bank")

        consts_loaded = sem("consts_loaded")
        consts2_loaded = sem("consts2_loaded")
        minus_half_set = sem("minus_half_set")
        k_padded, q_padded, v_padded = sem("k_padded"), sem("q_padded"), sem("v_padded")
        weights_rounded, weights_split = sem("weights_rounded"), sem("weights_split")
        xnT_full_done, xnT_done = sem("xnT_full_done"), sem("xnT_done")
        x_loaded = sem("x_loaded")
        xres_loaded = sem("xres_loaded")
        stats_done = sem("stats_done")
        moments_done = sem("moments_done")
        var_eps_done = sem("var_eps_done")
        rstd_done = sem("rstd_done")
        xn_done = sem("xn_done")
        v_filled, v_free = sem("v_filled"), sem("v_free")
        a_filled, a_free = sem("a_filled"), sem("a_free")
        gu_filled = sem("gu_filled")
        tanh_done = sem("tanh_done")
        act_done = sem("act_done")
        hidden_u_done = sem("hidden_u_done")
        hidden_done = sem("hidden_done")
        down_done = sem("down_done")
        pv_done = sem("pv_done")
        heads_t_done = sem("heads_t_done")
        den_done = sem("den_done")
        partial_done = sem("partial_done")
        stored = sem("stored")
        split_step = sem("split_step")
        parts_done = sem("parts_done")
        parts_stored = sem("parts_stored")
        rows_loaded = sem("rows_loaded")
        shift_hi_done = sem("shift_hi_done")
        shift_done = sem("shift_done")
        shift_stored = sem("shift_stored")
        shift_loaded = sem("shift_loaded")
        top_done = sem("top_done")
        top_at_done = sem("top_at_done")
        picks_done = sem("picks_done")
        gap_done = sem("gap_done")
        gap_exp_done = sem("gap_exp_done")
        gap_step = sem("gap_step")
        gates_done = sem("gates_done")
        gates_stored = sem("gates_stored")
        gates_loaded = sem("gates_loaded")

        V, A = Ring(V_ORDER), Ring(A_ORDER)
        STORES = 3
        SPLIT = 4

        def iterations(eng, iteration):
            def one(it):
                iteration(it, it % DEPTH, [s for s in STAGES if has((s,), it)])
            for it in range(FIRST, LOOP_FROM):
                one(it)
            trips = (FULL[1] - LOOP_FROM + 1) // DEPTH
            end = LOOP_FROM + trips * DEPTH
            with eng.Fori(LOOP_FROM, end - DEPTH + 1, DEPTH) as i:
                for j in range(DEPTH):
                    iteration(i + j if j else i, (LOOP_FROM + j) % DEPTH, list(STAGES))
            for it in range(end, LAST + 1):
                one(it)

        def static_before(ring, it):
            return ring.before(it) if isinstance(it, int) else ring.before_full

        assert V.full % 2 == 0 and A.full % 2 == 0

        block = ctx.enter_context(nc.Block())

        @block.tensor
        def _(pe):
            mm = nc.tensor.matmul

            def iteration(it, phase, stages):
                norm, prep, scan, main, tail = (s in stages for s in STAGES)
                bp, bs, bm, bt = (phase + 2) % DEPTH, (phase + 1) % DEPTH, phase, (phase - 1) % DEPTH

                def v_fill(name):
                    n = V.fill(name, it, stages)
                    if due(n - 1):
                        pe.wait_ge(v_free, n - 1)
                    return v_bank[V.bank(name, stages, static_before(V, it))]

                def a_fill(name):
                    n = A.fill(name, it, stages)
                    if due(n - 1):
                        pe.wait_ge(a_free, n - 1)
                    return a_bank[A.bank(name, stages, static_before(A, it))]

                def project(dst, w, x):
                    for n, (i, j) in enumerate(PASSES):
                        last = mm(dst, w[i], x[j], start=(n == 0), stop=(n == len(PASSES) - 1))
                    return last

                def weighted_values(h, buf, seq):
                    quad, j = h // 4, h % 4
                    if h % 8 == 0 and due(2 * seq + h // 8):
                        pe.wait_ge(heads_t_done, 2 * seq + h // 8)
                    for t in range(T):
                        last = mm(pv_bank[32 * j:32 * j + 32, quad % 2 * S:quad % 2 * S + S],
                                  values[:, buf, t, h, :], probs[:, h % PB, t, :],
                                  start=(t == 0), stop=(t == T - 1))
                    last.then_inc(pv_done, 1)

                def down(ch, seq):
                    if ch == 0 and due(seq):
                        pe.wait_ge(partial_done, seq)
                    pe.wait_ge(hidden_done, CHUNKS * seq + ch + 1)
                    for t in range(T):
                        last = mm(y_bank[:, t * D:(t + 1) * D], hidden[:, ch, t * P:(t + 1) * P], wd[:, ch, :],
                                  start=(ch == 0 and t == 0), stop=(ch == CHUNKS - 1), skip_group_check=True)
                    last.then_inc(down_done, 1)

                for s in range(H):
                    if main:
                        if s == 0:
                            pe.wait_ge(shift_loaded, 16 * (2 * it + 1))
                        if s == H // 2:
                            pe.wait_ge(shift_loaded, 16 * (2 * it + 2))
                        dst = a_fill(f"e{s}")
                        n = SLOT_ROWS + SHIFT_ROWS
                        for t in range(T):
                            last = mm(dst[:, t * S:(t + 1) * S], krows[bm][0:n, s, t * P:(t + 1) * P],
                                      qrows[bm][0:n, s, :], start=True, stop=True)
                        last.then_inc(a_filled, 1)
                    if scan:
                        if s == 0:
                            pe.wait_ge(rows_loaded, 16 * len(SETS) * (it + 2))
                        dst = v_fill(f"s{s}")
                        for t in range(T):
                            last = mm(dst[:, t * S:(t + 1) * S], qrows[bs][0:SLOT_ROWS, s, t * P:(t + 1) * P],
                                      krows[bs][0:SLOT_ROWS, s, :], start=True, stop=True)
                        last.then_inc(v_filled, 1)
                    if tail and s < 2:
                        pe.wait_ge(a_free, A.behind(f"e{H - 2 + s}", it))
                        weighted_values(H - 2 + s, bt, it - 1)
                    if main and s >= 2:
                        pe.wait_ge(a_free, A.fill(f"e{s - 2}", it, stages) + 1)
                        weighted_values(s - 2, bm, it)
                    if main and s in CHUNK_IN:
                        ch = CHUNK_IN[s]
                        if is_at(it, 0) and s == 0:
                            pe.wait_ge(weights_split, 2)
                        if due(CHUNKS * it + ch - 1):
                            pe.wait_ge(hidden_u_done, CHUNKS * it + ch - 1)
                        for g in range(2):
                            last = project(gu_bank[ch % 2][:, g * S:(g + 1) * S], [w[:, ch, g, :] for w in wgu],
                                           [part[:, bm, :] for part in xnT])
                        last.then_inc(gu_filled, 1)
                    if tail and s == LAST_DOWN_SLOT:
                        down(CHUNKS - 1, it - 1)
                    if main and s - 3 in CHUNK_IN:
                        down(CHUNK_IN[s - 3], it)

                    if prep and s == 0:
                        pe.wait_ge(xn_done, T * (it + 3))
                        if is_at(it, -2):
                            pe.wait_ge(consts_loaded, 16)
                        dst = a_fill("xnT")
                        for t in range(T):
                            last = nc.tensor.transpose(dst[:, t * P:(t + 1) * P], xn[:, t, :], ident)
                        last.then_inc(a_filled, 1)
                    if main and s == 1:
                        pe.wait_ge(v_free, V.behind(f"s{H - 1}", it))
                        dst = v_fill("max1")
                        nc.tensor.transpose(dst[0:H // 2 * T, 0:P], row_max[:, 1, :], ident).then_inc(v_filled, 1)
                    if prep and s in (2, 3):
                        if s == 2:
                            pe.wait_ge(xnT_done, it + 3)
                            if is_at(it, -2):
                                pe.wait_ge(weights_split, 1)
                        dst = v_fill(f"rope{s - 2}")
                        for m in range(2):
                            last = project(dst[:, m * S:(m + 1) * S], [w[:, 2 * m + s - 2, :] for w in wqk],
                                           [part[:, bp, :] for part in xnT])
                        last.then_inc(v_filled, 1)
                    if prep and s == 4:
                        dst = v_fill("vg")
                        for t in range(T):
                            last = project(dst[:, t * VG:(t + 1) * VG],
                                           [part[:, bp, t * P:(t + 1) * P] for part in xnT], wvg)
                        last.then_inc(v_filled, 1)
                    if tail and s in (5, 6):
                        if s == 5:
                            pe.wait_ge(heads_t_done, 2 * it)
                        t = s - 5
                        dst = v_fill(f"out{t}")
                        for quad in range(QUADS):
                            last = nc.tensor.transpose(dst[:, quad * P:(quad + 1) * P],
                                                       heads_t[:, quad, t * P:(t + 1) * P], ident)
                        last.then_inc(v_filled, 1)
                    if tail and s == 7:
                        pe.wait_ge(v_free, V.fill("out1", it, stages) + 1)
                        dst = a_fill("outT")
                        for t in range(T):
                            last = nc.tensor.transpose(dst[:, t * P:(t + 1) * P], heads[:, t, :], ident)
                        last.then_inc(a_filled, 1)
                    if (tail or scan) and s == 9:
                        dst = v_fill("wo_max0")
                        if scan:
                            pe.wait_ge(v_free, V.fill("s7", it, stages) + 1)
                            last = nc.tensor.transpose(dst[0:H // 2 * T, S:S + P], row_max[:, 0, :], ident)
                        if tail:
                            pe.wait_ge(a_free, A.fill("outT", it, stages) + 1)
                            for t in range(T):
                                last = mm(dst[:, t * D:(t + 1) * D], out_t[:, t * P:(t + 1) * P], wo,
                                          start=True, stop=True)
                        last.then_inc(v_filled, 1)
                    if prep and s == 11:
                        pe.wait_ge(gates_done, it + 3)
                        dst = v_fill("gates")
                        for t in range(T):
                            last = nc.tensor.transpose(dst[0:GATES, t * P:(t + 1) * P], gates[:, t, :], ident)
                        last.then_inc(v_filled, 1)

            iterations(pe, iteration)

        @block.scalar
        def _(act_e):
            act_fn = nc.scalar.activation

            def iteration(it, phase, stages):
                norm, prep, scan, main, tail = (s in stages for s in STAGES)
                bp = (phase + 2) % DEPTH

                def filled(name):
                    act_e.wait_ge(a_filled, A.fill(name, it, stages) + 1)
                    return a_bank[A.bank(name, stages, static_before(A, it))]

                def copy_heads(half, seq):
                    act_e.wait_ge(pv_done, H * seq + 8 * (half + 1))
                    act_fn(heads_t[:, 2 * half:2 * half + 2, :],
                           pv_bank[:, :].rearrange("p (q s) -> p q s", q=2), ACT.Copy).then_inc(heads_t_done, 1)

                for s in range(H):
                    if main:
                        src = filled(f"e{s}")
                        if due(H * it + s - PB + 1):
                            act_e.wait_ge(pv_done, H * it + s - PB + 1)
                        act_fn(probs[:, s % PB, :, :], src[:, :].rearrange("p (t s) -> p t s", t=T), ACT.Exp,
                               scale=SCALE).then_inc(a_free, 1)
                    if prep and s == 0:
                        src = filled("xnT")
                        if due(it + 2):
                            act_e.wait_ge(xnT_done, it + 2)
                        act_fn(xnT_full[:, :], src[:, 0:S], ACT.Copy).then_inc(xnT_full_done, 1)
                        act_fn(xnT[0][:, bp, :], src[:, 0:S], ACT.Copy).then_inc(a_free, 1)
                    if main and s in CHUNK_IN:
                        ch = CHUNK_IN[s]
                        act_e.wait_ge(gu_filled, CHUNKS * it + ch + 1)
                        if due(CHUNKS * it + ch - 1):
                            act_e.wait_ge(act_done, CHUNKS * it + ch - 1)
                        act_fn(tanh[:, ch % 2, :], gu_bank[ch % 2][:, 0:S], ACT.Tanh, scale=0.5)\
                            .then_inc(tanh_done, 1)
                    if tail and s == 1:
                        copy_heads(1, it - 1)
                    if main and s == 9:
                        copy_heads(0, it)
                    if prep and s == 7:
                        act_e.wait_ge(gap_done, 2 * (it + 3))
                        act_fn(gap_exp[:, :, :], gap[:, :, :], ACT.Exp).then_inc(gap_exp_done, 1)
                    if tail and s == 7:
                        src = filled("outT")
                        act_fn(out_t[:, :], src[:, 0:S], ACT.Copy).then_inc(a_free, 1)

            iterations(act_e, iteration)

        @block.vector
        def _(dve):
            v = nc.vector

            def pad_buffers(i):
                v.memset(krows[i][0:SLOT_ROWS, :, :].bitcast(F32), 0.0).then_inc(k_padded, 1)
                v.memset(krows[i][SLOT_ROWS:P, :, :].bitcast(F32), TWO_ONES).then_inc(k_padded, 1)
                v.memset(values[:, i, :, :, :], 0.0).then_inc(v_padded, 1)
                dve.wait_ge(v_padded, 2 * i + 1)
                v.memset(values[:, i, :, :, HD:HD + 1], 1.0).then_inc(v_padded, 1)

            def split_weights(first, end):
                high, low = (w[:, first - SPLIT_FROM:end - SPLIT_FROM] for w in weights)
                n = 1 if first == SPLIT_FROM else 2
                v.tensor_copy(high, const[:, first:end]).then_inc(weights_rounded, 1)
                dve.wait_ge(weights_rounded, n)
                v.tensor_tensor(low, const[:, first:end], high.bitcast(F32), ALU.subtract).then_inc(weights_split, 1)

            def iteration(it, phase, stages):
                norm, prep, scan, main, tail = (s in stages for s in STAGES)
                bp, bt = (phase + 2) % DEPTH, (phase - 1) % DEPTH
                sp, sn = it + 2, it + 3

                def filled(name):
                    dve.wait_ge(v_filled, V.fill(name, it, stages) + 1)
                    return v_bank[V.bank(name, stages, static_before(V, it))]

                def shifts(half, src, n, last):
                    if due(n - 1):
                        dve.wait_ge(shift_stored, 16 * (n - 1))
                    v.tensor_scalar(shift[:, half, 0, :], src, -1.0, None, ALU.mult).then_inc(shift_hi_done, 1)
                    dve.wait_ge(shift_hi_done, n + 1)
                    v.scalar_tensor_tensor(out=shift[:, half, 1, :], in0=src, scalar=-1.0,
                                           in1=shift[:, half, 0, :], op0=ALU.mult, op1=ALU.subtract)\
                        .then_inc(last, 1)

                if is_at(it, FIRST):
                    v.memset(minus_half[:, :], -0.5).then_inc(minus_half_set, 1)
                for s in range(H):
                    if main and s - 1 in CHUNK_IN:
                        ch = CHUNK_IN[s - 1]
                        n = CHUNKS * it + ch
                        dve.wait_ge(tanh_done, n + 1)
                        if due(n - 1):
                            dve.wait_ge(hidden_u_done, n - 1)
                        v.scalar_tensor_tensor(out=act[:, ch % 2, :], in0=tanh[:, ch % 2, :], scalar=1.0,
                                               in1=gu_bank[ch % 2][:, 0:S], op0=ALU.add, op1=ALU.mult)\
                            .then_inc(act_done, 1)
                    if prep and s == 5:
                        dve.wait_ge(v_free, V.fill("vg", it, stages) + 1)
                    if prep and s == 6:
                        dve.wait_ge(top_done, T * (sp + 1))
                    if norm and s == 9:
                        dve.wait_ge(stats_done, T * (sn + 1))
                    if scan:
                        src = filled(f"s{s}")
                        at = s % 8 * T
                        if s == 0 and due(V.behind("wo_max0", it)):
                            dve.wait_ge(v_filled, V.behind("wo_max0", it))
                        if s == 8 and main:
                            dve.wait_ge(v_filled, V.fill("max1", it, stages) + 1)
                        v.tensor_reduce(row_max[:, s // 8, at:at + T], src[:, :].rearrange("p (t k) -> p t k", t=T),
                                        AX_X, ALU.max).then_inc(v_free, 1)
                    if main and s - 1 in CHUNK_IN:
                        dve.wait_ge(act_done, n + 1)
                        if due(n - HU + 1):
                            dve.wait_ge(hidden_done, n - HU + 1)
                        v.tensor_tensor(hidden_u[:, ch % HU, :], act[:, ch % 2, :],
                                        gu_bank[ch % 2][:, S:2 * S], ALU.mult).then_inc(hidden_u_done, 1)

                    if main and s == 1:
                        shifts(1, filled("max1")[0:H // 2 * T, 0:P], 2 * it + 1, v_free)
                    if prep and s == 2:
                        if is_at(it, -2):
                            dve.wait_ge(consts_loaded, 16)
                        src = filled("rope0")[:, :].rearrange("p (m s) -> p m s", m=2)
                        if due(sp):
                            dve.wait_ge(split_step, SPLIT * sp)
                        v.tensor_tensor(rope_c[:, :, :], src, cos.unsqueeze(1).to_broadcast([P, 2, S]),
                                        ALU.mult).then_inc(v_free, 1)
                    if tail and s == 2:
                        dve.wait_ge(down_done, CHUNKS * it)
                        dve.wait_ge(xres_loaded, 16 * it)
                        v.tensor_tensor(partial[:, :, :], y_bank[:, 0:T * D].rearrange("p (t d) -> p t d", t=T),
                                        xres[:, bt, :, :], ALU.add).then_inc(partial_done, 1)
                    if prep and s == 3:
                        src = filled("rope1")[:, :].rearrange("p (m s) -> p m s", m=2)
                        v.tensor_tensor(rope_s[:, :, :], src, sin.unsqueeze(1).to_broadcast([P, 2, S]),
                                        ALU.mult).then_inc(v_free, 1)
                    if prep and s == 4:
                        src = filled("vg")[:, 0:T * VG].rearrange("p (t c) -> p t c", t=T)
                        if it in (-2, -1, 0) if isinstance(it, int) else False:
                            dve.wait_ge(v_padded, 2 * (sp + 1))
                        for t in range(T):
                            v.tensor_copy(values[:, bp, t, :, 0:HD],
                                          src[:, t, 0:D].rearrange("p (h d) -> p h d", d=HD))
                        if due(sp):
                            dve.wait_ge(gates_done, sp)
                        v.tensor_copy(logits[:, :, :], src[:, :, D:D + GATES]).then_inc(v_free, 1)
                    if prep and s == 5:
                        for t in range(T):
                            v.max(top[:, t, :], logits[:, t, 0:E]).then_inc(top_done, 1)
                    if prep and s == 6:
                        for t in range(T):
                            v.max_index(top_at[:, t, :], top[:, t, :], logits[:, t, 0:E]).then_inc(top_at_done, 1)
                        v.tensor_tensor(gap[:, :, 0], top[:, :, 1], top[:, :, 0], ALU.subtract).then_inc(gap_done, 1)
                        v.tensor_scalar(gap[:, :, 1], logits[:, :, E], -1.0, None, ALU.mult).then_inc(gap_done, 1)
                    if tail and s in (5, 6):
                        t = s - 5
                        src = filled(f"out{t}")[:, :].rearrange("p (h r) -> p h r", r=HPAD)
                        v.reciprocal(den_rec[:, t, :], src[:, :, HD]).then_inc(den_done, 1)
                        if t == 0 and due(A.behind("outT", it)):
                            dve.wait_ge(a_filled, A.behind("outT", it))
                        dve.wait_ge(den_done, T * (it - 1) + t + 1)
                        v.tensor_tensor(heads[:, t, :].rearrange("p (h d) -> p h d", d=HD), src[:, :, 0:HD],
                                        den_rec[:, t, :].unsqueeze(2).to_broadcast([P, H, HD]),
                                        ALU.mult).then_inc(v_free, 1)
                    if prep and s == 7:
                        dve.wait_ge(top_at_done, T * (sp + 1))
                        v.tensor_copy(top_atf[:, :, :], top_at[:, :, 0:2]).then_inc(gap_step, 1)
                    if norm and s == 8:
                        dve.wait_ge(x_loaded, 16 * (sn + 1))
                        for t in range(T):
                            v.bn_stats(stats[:, t, :], xin[:, phase, t, :]).then_inc(stats_done, 1)
                    if prep and s == 8:
                        dve.wait_ge(gap_exp_done, sp + 1)
                        v.tensor_scalar(gap_one[:, :, :], gap_exp[:, :, :], 1.0, None, ALU.add).then_inc(gap_step, 1)
                        dve.wait_ge(gap_step, 5 * sp + 2)
                        v.reciprocal(gap_rec[:, :, :], gap_one[:, :, :]).then_inc(gap_step, 1)
                        dve.wait_ge(gap_step, 5 * sp + 3)
                        v.tensor_scalar(first_w[:, :, :], gap_rec[:, :, :], 0.5, None, ALU.mult).then_inc(gap_step, 1)
                    if norm and s == 9:
                        for t in range(T):
                            v.bn_aggr(moments[:, t, :], stats[:, t, :]).then_inc(moments_done, 1)
                    if (tail or scan) and s == 9:
                        src = filled("wo_max0")
                        if scan:
                            shifts(0, src[0:H // 2 * T, S:S + P], 2 * (it + 1), shift_done if tail else v_free)
                    if tail and s == 9:
                        if due(it - 1):
                            dve.wait_ge(stored, 16 * (it - 1))
                        v.tensor_tensor(result[:, :, :], src[:, 0:T * D].rearrange("p (t d) -> p t d", t=T),
                                        partial[:, :, :], ALU.add).then_inc(v_free, 1)
                    if prep and s == 9:
                        dve.wait_ge(gap_step, 5 * sp + 4)
                        v.tensor_tensor(second_w[:, :, :], gap_exp[:, :, 0:1], first_w[:, :, 0:1], ALU.mult)\
                            .then_inc(gap_step, 1)
                        for t in range(T):
                            v.tensor_scalar(pick_a[:, t, :], c("iota"), top_atf[:, t, 0:1], first_w[:, t, 0:1],
                                            ALU.is_equal, ALU.mult).then_inc(picks_done, 1)
                        dve.wait_ge(gap_step, 5 * sp + 5)
                        for t in range(T):
                            v.tensor_scalar(pick_b[:, t, :], c("iota"), top_atf[:, t, 1:2], second_w[:, t, 0:1],
                                            ALU.is_equal, ALU.mult).then_inc(picks_done, 1)
                        if due(V.behind("gates", it)):
                            dve.wait_ge(v_filled, V.behind("gates", it))
                        v.tensor_copy(gates[:, :, E:GATES], first_w[:, :, 1:2]).then_inc(picks_done, 1)
                        dve.wait_ge(picks_done, 5 * (sp + 1))
                        v.tensor_tensor(gates[:, :, 0:E], pick_a[:, :, :], pick_b[:, :, :], ALU.add)\
                            .then_inc(gates_done, 1)
                    if norm and s == 10:
                        dve.wait_ge(moments_done, T * (sn + 1))
                        v.tensor_scalar(var_eps[:, :], moments[:, :, 1], EPS, None, ALU.add).then_inc(var_eps_done, 1)
                    if prep and s == 11:
                        src = filled("gates")
                        if due(sp):
                            dve.wait_ge(gates_stored, 16 * sp)
                        v.tensor_copy(gates_t[0:GATES, :], src[0:GATES, 0:S]).then_inc(v_free, 1)
                    if norm and s == 12:
                        dve.wait_ge(rstd_done, sn + 1)
                        if prep:
                            dve.wait_ge(a_filled, A.fill("xnT", it, stages) + 1)
                        for t in range(T):
                            v.tensor_scalar(xn[:, t, :], xin[:, phase, t, :], moments[:, t, 0:1], rstd[:, t:t + 1],
                                            ALU.subtract, ALU.mult).then_inc(xn_done, 1)
                    if it in (-3, -2, -1) if isinstance(it, int) else False:
                        if s == 13:
                            pad_buffers(it + 3)
                        if s == 12 and it == -3:
                            dve.wait_ge(consts_loaded, 16)
                            split_weights(SPLIT_FROM, COLS["wgu"][0])
                        if s == 12 and it == -1:
                            dve.wait_ge(consts2_loaded, 16)
                            split_weights(COLS["wgu"][0], CONST_COLS)

            iterations(dve, iteration)

        @block.gpsimd
        def _(pool):
            g = nc.gpsimd

            def iteration(it, phase, stages):
                norm, prep, scan, main, tail = (s in stages for s in STAGES)
                bp = (phase + 2) % DEPTH
                sp = it + 2
                if it < 0 if isinstance(it, int) else False:
                    g.memset(qrows[it + 3][:, :, :].bitcast(F32), 0.0).then_inc(q_padded, 1)
                for s in range(H):
                    if prep and s == 0:
                        pool.wait_ge(xnT_full_done, sp + 1)
                        pool.wait_ge(a_free, A.fill("xnT", it, stages) + 1)
                        g.tensor_tensor(xnT[1][:, bp, :], xnT_full[:, :], xnT[0][:, bp, :].bitcast(F32),
                                        ALU.subtract).then_inc(xnT_done, 1)
                    if scan and s == 6:
                        pool.wait_ge(gates_loaded, 16 * 3 * (it + 2))
                    if main and s - 1 in CHUNK_IN:
                        ch = CHUNK_IN[s - 1]
                        pool.wait_ge(hidden_u_done, CHUNKS * it + ch + 1)
                        if due(CHUNKS * (it - 1) + ch + 1):
                            pool.wait_ge(down_done, CHUNKS * (it - 1) + ch + 1)
                        g.tensor_tensor(hidden[:, ch, :], hidden_u[:, ch % HU, :],
                                        gates_b[phase][:, min(ch, PAIRS), :], ALU.mult).then_inc(hidden_done, 1)
                    if prep and s == 4:
                        pool.wait_ge(v_free, V.fill("rope1", it, stages) + 1)
                        if due(sp):
                            pool.wait_ge(parts_done, sp)
                        g.tensor_tensor(qk[:, :, :], rope_c[:, :, :], rope_s[:, :, :], ALU.add)\
                            .then_inc(split_step, 1)
                        if due(sp):
                            pool.wait_ge(parts_stored, 16 * STORES * sp)
                        g.tensor_tensor(parts[:, PART_AT[0], :], rope_c[:, :, :], rope_s[:, :, :], ALU.add)\
                            .then_inc(split_step, 1)
                    if prep and s == 5:
                        pool.wait_ge(split_step, SPLIT * sp + 2)
                        g.tensor_tensor(parts[:, PART_AT[1], :], qk[:, :, :], parts[:, PART_AT[0], :], ALU.subtract)\
                            .then_inc(split_step, 1)
                    if prep and s == 6:
                        g.tensor_tensor(qk_rest[:, :, :], qk[:, :, :], parts[:, PART_AT[0], :], ALU.subtract)\
                            .then_inc(split_step, 1)
                        pool.wait_ge(split_step, SPLIT * sp + 4)
                        g.tensor_tensor(parts[:, PART_AT[2], :], qk_rest[:, :, :], parts[:, PART_AT[1], :], ALU.subtract)\
                            .then_inc(parts_done, 1)
                    if norm and s == 10:
                        if is_at(it, FIRST):
                            pool.wait_ge(minus_half_set, 1)
                        pool.wait_ge(var_eps_done, it + 4)
                        if due(it + 3):
                            pool.wait_ge(xn_done, T * (it + 3))
                        g.tensor_tensor(rstd[:, :], var_eps[:, :], minus_half[:, :], ALU.pow).then_inc(rstd_done, 1)

            iterations(pool, iteration)

        @block.sync
        def _(sp_e):
            dma = sp_e.dma_start

            def rows_of(ap, seq):
                return ap[seq].rearrange("(p t) d -> p t d", t=T)

            def iteration(it, phase, stages):
                norm, prep, scan, main, tail = (s in stages for s in STAGES)
                bp, bs, bm, bt = (phase + 2) % DEPTH, (phase + 1) % DEPTH, phase, (phase - 1) % DEPTH
                seq = it + 2

                def store_shifts(half, fill, buf):
                    sp_e.wait_ge(v_free, V.fill(fill, it, stages) + 1)
                    dma(shift_dram[buf, half], shift[:, half, :, :]).then_inc(shift_stored, 16)

                def load_shifts(half, n, buf):
                    sp_e.wait_ge(shift_stored, 16 * (n + 1))
                    cols = slice(half * H // 2, (half + 1) * H // 2)
                    dma(qrows[buf][SLOT_ROWS:SLOT_ROWS + SHIFT_ROWS, cols, :].rearrange("r h (t q) -> r (h t) q", t=T),
                        shift_dram[buf, half].rearrange("c r q -> r c q")).then_inc(shift_loaded, 16)

                if norm:
                    if due(it + 3):
                        sp_e.wait_ge(xn_done, T * (it + 3))
                    dma(xin[:, phase, :, :], rows_of(x, it + 3)).then_inc(x_loaded, 16)
                if is_at(it, FIRST):
                    dma(const[:, 0:SMALL_COLS], consts[:, 0:SMALL_COLS]).then_inc(consts_loaded, 16)
                    dma(const[:, SMALL_COLS:], consts[:, SMALL_COLS:]).then_inc(consts2_loaded, 16)
                if main:
                    store_shifts(1, "max1", bm)
                    load_shifts(1, 2 * it + 1, bm)
                    if due(it):
                        sp_e.wait_ge(partial_done, it)
                    dma(xres[:, bm, :, :], rows_of(x, it)).then_inc(xres_loaded, 16)
                if prep:
                    def scratch(i, first, count):
                        return parts_dram[bp, i, :, :, first:first + count, :].rearrange("m p j c -> p m j c")

                    sp_e.wait_ge(parts_done, seq + 1)
                    for i, first, count, held in ((0, 0, 3, slice(0, 6)), (1, 0, 2, slice(1, 5)), (1, 2, 1, slice(2, 4))):
                        dma(scratch(i, first, count), parts[:, held, :].rearrange("p (m j) c -> p m j c", m=2))\
                            .then_inc(parts_stored, 16)
                    if it < 1 if isinstance(it, int) else False:
                        sp_e.wait_ge(q_padded, seq + 1)
                        sp_e.wait_ge(k_padded, 2 * (seq + 1))
                    sp_e.wait_ge(parts_stored, 16 * STORES * (seq + 1))
                    for i in range(len(SETS)):
                        dma(rows[bp][i * SET_ROWS:(i + 1) * SET_ROWS].rearrange("r m h c -> r (m h) c"),
                            parts_dram[bp, i].rearrange("m (h d) j c -> (d j) (m h) c", d=HD)).then_inc(rows_loaded, 16)
                if scan:
                    store_shifts(0, "wo_max0", bs)
                if tail:
                    if not scan:
                        sp_e.wait_ge(v_free, V.fill("wo_max0", it, stages) + 1)
                    dma(rows_of(out, it - 1), result[:, :, :]).then_inc(stored, 16)
                if scan:
                    load_shifts(0, 2 * (it + 1), bs)
                if prep:
                    sp_e.wait_ge(v_free, V.fill("gates", it, stages) + 1)
                    dma(gates_dram[bp], gates_t[0:GATES, :]).then_inc(gates_stored, 16)
                    sp_e.wait_ge(gates_stored, 16 * (seq + 1))
                    for half in range(2):
                        dma(gates_b[bp][half * EH:(half + 1) * EH, 0:PAIRS, :],
                            gates_dram[bp, half:E:2, :].partition_broadcast(EH)).then_inc(gates_loaded, 16)
                    dma(gates_b[bp][:, PAIRS, :], gates_dram[bp, E, :].partition_broadcast(P))\
                        .then_inc(gates_loaded, 16)

            iterations(sp_e, iteration)
            sp_e.wait_ge(stored, 16 * B)


def constants():
    token = (T * np.arange(P)[None, :] + np.arange(T)[:, None]).reshape(S).astype(np.float32)
    inv = (1.0 / 10000.0 ** (np.arange(0, HD, 2, dtype=np.float32) / HD)).astype(np.float32)
    angle = inv[:, None] * token[None, :]
    cos = np.tile(np.repeat(np.cos(angle), 2, axis=0), (H, 1))
    sin = np.tile(np.stack([-np.sin(angle), np.sin(angle)], axis=1).reshape(HD, S), (H, 1))
    return np.eye(P, dtype=np.float32), np.tile(np.arange(E, dtype=np.float32), (P, 1)), \
        cos.astype(np.float32), sin.astype(np.float32)


def kernel(L0_attn_x, L0_attn_wq, L0_attn_wk, L0_attn_wv, L0_attn_wo, L0_ffn_Wg, L0_ffn_We_gate, L0_ffn_We_up,
           L0_ffn_We_down, L0_ffn_Ws_gate, L0_ffn_Ws_up, L0_ffn_Ws_down, L0_ffn_Wsg):
    import concourse.bacc as bacc
    from concourse.bass_utils import run_bass_kernel_spmd

    ident, iota, cos, sin = constants()
    swap = np.arange(D).reshape(D // 2, 2)[:, ::-1].reshape(D)
    a = [np.asarray(w) for w in (L0_attn_wq, L0_attn_wk, L0_attn_wv, L0_attn_wo, L0_ffn_Wg, L0_ffn_Wsg)]
    wq, wk, wv, wo, wg, wsg = a
    eg, eu, ed, sg, su, sd = [np.asarray(w) for w in (L0_ffn_We_gate, L0_ffn_We_up, L0_ffn_We_down,
                                                      L0_ffn_Ws_gate, L0_ffn_Ws_up, L0_ffn_Ws_down)]
    gate = np.concatenate([eg.reshape(E * EH, D), sg]).reshape(CHUNKS, P, D)
    up = np.concatenate([eu.reshape(E * EH, D), su]).reshape(CHUNKS, P, D)
    gate_up = np.stack([gate, up], axis=1).transpose(3, 0, 1, 2).reshape(D, CHUNKS * 2 * P)
    down = np.concatenate([ed.transpose(0, 2, 1).reshape(E * EH, D), sd.T]).reshape(CHUNKS, P, D)
    down = down.transpose(1, 0, 2).reshape(P, CHUNKS * D)
    consts = np.concatenate([ident, iota, cos, sin, wo.T, down, wq.T, wq[swap].T, wk.T, wk[swap].T, wv.T, wg.T,
                             wsg.T, np.zeros((D, VG - D - GATES), wv.dtype), gate_up], axis=1)
    arrays = {"x": np.ascontiguousarray(L0_attn_x), "consts": np.ascontiguousarray(consts)}

    nc = bacc.Bacc("TRN2", target_bir_lowering=False, num_devices=1)
    x_ap = nc.dram_tensor("x", (B, S, D), F32, kind="ExternalInput").ap()
    c_ap = nc.dram_tensor("consts", (P, CONST_COLS), F32, kind="ExternalInput").ap()
    o_ap = nc.dram_tensor("out", (B, S, D), F32, kind="ExternalOutput").ap()
    build(nc, x_ap, c_ap, o_ap)
    r = run_bass_kernel_spmd(nc, [arrays], core_ids=[0])
    return r.results[0]["out"]
```

```python
from contextlib import ExitStack

import numpy as np

import concourse.bass as bass
from concourse import mybir

F32 = mybir.dt.float32
BF16 = mybir.dt.bfloat16
F32R = mybir.dt.float32r
U32 = mybir.dt.uint32
ALU = mybir.AluOpType
ACT = mybir.ActivationFunctionType
AX_X = mybir.AxisListType.X

P = 128
B, S, D = 32, 256, 128
T = S // P
H, HD = 16, 8
E, EH = 16, 64
SH = 256
PAIRS = E * EH // P
CHUNKS = PAIRS + SH // P
VG = D + E + 2
GATES = E + 1
QUADS = H // 4
HPAD = 32
SCALE = float(1.0 / np.sqrt(HD))
EPS = 1e-5
TWO_ONES = float(np.array([0x3F803F80], np.uint32).view(np.float32)[0])

SETS = (((2, 0), (1, 1), (0, 2)), ((1, 0), (0, 1), (0, 0)))
PARTS = 3
SET_ROWS = PARTS * HD
PART_AT = (slice(2, 4), slice(1, 5, 3), slice(0, 6, 5))
SLOT_ROWS = 96
SHIFT_ROWS = 2


COLS = {}
_at = 0
for _name, _n in (("ident", P), ("iota", E), ("cos", S), ("sin", S), ("wvg", VG),
                  ("wqk", 4 * D), ("wgu", CHUNKS * 2 * P), ("wo", D), ("wd", CHUNKS * D)):
    COLS[_name] = (_at, _at + _n)
    _at += _n
CONST_COLS = _at
SPLIT_FROM = COLS["wqk"][0]
SPLIT_END = COLS["wgu"][1]
SMALL_COLS = COLS["wgu"][0]

NORM, PREP, SCAN, MAIN, TAIL = "NORM", "PREP", "SCAN", "MAIN", "TAIL"
RUNS_IN = {NORM: (-3, B - 4), PREP: (-2, B - 3), SCAN: (-1, B - 2), MAIN: (0, B - 1), TAIL: (1, B)}
STAGES = (NORM, PREP, SCAN, MAIN, TAIL)
FIRST, LAST = -3, B
FULL = (1, B - 4)
LOOP_FROM = 2
DEPTH = 3

CHUNK_SLOT = [c * H // CHUNKS for c in range(CHUNKS)]
DOWN_AFTER = 4
CHUNK_IN = {s: c for c, s in enumerate(CHUNK_SLOT)}

ROPE_SLOT, VG_SLOT = 2, 4
MAX1_SLOT, MAX0_SLOT = 3, 10
OUT_SLOT, WO_SLOT = 5, 13
QUAD_SLOTS = (5, 9, 13)

V_EXTRA = {ROPE_SLOT: ("rope0", (PREP,)), ROPE_SLOT + 1: ("rope1", (PREP,)), OUT_SLOT: ("out0", (TAIL,)),
           OUT_SLOT + 1: ("out1", (TAIL,)), WO_SLOT: ("wo0", (TAIL,)), WO_SLOT + 1: ("wo1", (TAIL,))}
V_ORDER = [x for h in range(H) for x in [(f"s{h}", (SCAN,))] + ([V_EXTRA[h]] if h in V_EXTRA else [])]
A_EXTRA = {MAX1_SLOT: ("max1_gates", (MAIN, SCAN)), VG_SLOT: ("vg", (PREP,)),
           MAX0_SLOT: ("max0_outT", (SCAN, TAIL)), H - 1: ("xnT", (NORM,))}
A_ORDER = [x for h in range(H) for x in [(f"e{h}", (MAIN,))] + ([A_EXTRA[h]] if h in A_EXTRA else [])]


def has(stages, it):
    return any(RUNS_IN[stage][0] <= it <= RUNS_IN[stage][1] for stage in stages)


def is_at(it, *iterations):
    return isinstance(it, int) and it in iterations


class Ring:

    def __init__(self, order):
        self.order = order
        self.full = len(order)
        self.before_full = self._before(FULL[0])

    def _before(self, it):
        return sum(sum(has(of, j) for _, of in self.order) for j in range(FIRST, it))

    def before(self, it):
        if isinstance(it, int) and not FULL[0] <= it <= FULL[1] + 1:
            return self._before(it)
        return (it - FULL[0]) * self.full + self.before_full

    def index(self, name, stages):
        return [n for n, of in self.order if set(of) & set(stages)].index(name)

    def fill(self, name, it, stages):
        return self.before(it) + self.index(name, stages)

    def bank(self, name, stages, static_before):
        return (static_before + self.index(name, stages)) % 2

    def behind(self, name, it):
        if isinstance(it, int):
            before = [n for n, of in self.order if has(of, it - 1)]
            return self._before(it - 1) + before.index(name) + 1 if name in before else 0
        return self.before(it) - self.full + [n for n, _ in self.order].index(name) + 1


def due(count):
    return not isinstance(count, int) or count > 0


def build(nc, x, consts, out):
    with ExitStack() as ctx:
        def sb(name, shape, dt=F32):
            return ctx.enter_context(nc.sbuf_tensor(name, shape, dt))

        def bank(name):
            return ctx.enter_context(nc.psum_tensor(name, [P, 512], F32))

        def sem(name):
            return ctx.enter_context(nc.semaphore(name))

        parts_dram = nc.dram_tensor("parts_dram", (DEPTH, len(SETS), 2, P, PARTS, S), BF16, kind="Internal").ap()
        shift_dram = nc.dram_tensor("shift_dram", (DEPTH, 2, SHIFT_ROWS, H // 2 * T, P), BF16, kind="Internal").ap()
        gates_dram = nc.dram_tensor("gates_dram", (DEPTH, GATES, S), F32, kind="Internal").ap()

        const = sb("const", [P, CONST_COLS])

        def c(name):
            return const[:, COLS[name][0]:COLS[name][1]]

        ident, wo = c("ident"), c("wo")
        ident_bf = sb("ident_bf", [P, P], BF16)
        weights = [sb(f"weights_{part}", [P, SPLIT_END - SPLIT_FROM], F32R) for part in ("high", "low")]

        def split(name):
            return [w[:, COLS[name][0] - SPLIT_FROM:COLS[name][1] - SPLIT_FROM] for w in weights]

        wqk = [w.rearrange("p (m o) -> p m o", m=4) for w in split("wqk")]
        wgu = [w.rearrange("p (c g o) -> p c g o", c=CHUNKS, g=2) for w in split("wgu")]
        PASSES = ((0, 0), (0, 1), (1, 0))
        wd = c("wd").rearrange("p (c o) -> p c o", c=CHUNKS)
        cos, sin = c("cos"), c("sin")

        xin = sb("xin", [P, DEPTH, T, D])
        xres = sb("xres", [P, DEPTH, T, D])
        xnT_full = sb("xnT_full", [P, S])
        xnT = [sb(f"xnT_{part}", [P, DEPTH, S], F32R) for part in ("high", "low")]
        rows = [sb(f"rows{i}", [P, 2, H, S], BF16) for i in range(DEPTH)]
        qrows, krows = [r[:, 0] for r in rows], [r[:, 1] for r in rows]
        values = sb("values", [P, DEPTH, T, H, HPAD])
        gates_b = [sb(f"gates_b{i}", [P, PAIRS + 1, S]) for i in range(DEPTH)]
        stats = sb("stats", [P, T, 6])
        moments = sb("moments", [P, T, 2])
        var_eps = sb("var_eps", [P, T])
        minus_half = sb("minus_half", [P, T])
        rstd = sb("rstd", [P, T])
        xn = sb("xn", [P, T, D])
        logits = sb("logits", [P, T, GATES])
        top = sb("top", [P, T, 8])
        top_at = sb("top_at", [P, T, 8], U32)
        top_atf = sb("top_atf", [P, T, 2])
        gap = sb("gap", [P, T, 2])
        gap_exp = sb("gap_exp", [P, T, 2])
        gap_one = sb("gap_one", [P, T, 2])
        gap_rec = sb("gap_rec", [P, T, 2])
        first_w = sb("first_w", [P, T, 2])
        second_w = sb("second_w", [P, T, 1])
        pick_a = sb("pick_a", [P, T, E])
        pick_b = sb("pick_b", [P, T, E])
        gates = sb("gates", [P, T, GATES])
        gates_t = sb("gates_t", [32, S])
        rope_c = sb("rope_c", [P, 2, S])
        rope_s = sb("rope_s", [P, 2, S])
        qk = sb("qk", [P, 2, S])
        qk_rest = sb("qk_rest", [P, 2, S])
        parts = sb("parts", [P, 2 * PARTS, S], BF16)
        row_max = sb("row_max", [P, 2, H // 2 * T])
        neg_max = sb("neg_max", [P, 2, SHIFT_ROWS, H // 2 * T], BF16)
        shift = sb("shift", [SHIFT_ROWS * H // 2 * T, 2, P], BF16)
        PB = 8
        probs = sb("probs", [P, PB, T, S])
        heads_t = sb("heads_t", [P, QUADS, S])
        den_rec = sb("den_rec", [P, T, H])
        heads = sb("heads", [P, T, D])
        out_t = sb("out_t", [P, S])
        tanh = sb("tanh", [P, 2, S])
        act = sb("act", [P, 2, S])
        HU = 5
        hidden_u = sb("hidden_u", [P, HU, S])
        hidden = sb("hidden", [P, CHUNKS, S])
        partial = sb("partial", [P, T, D])
        result = sb("result", [P, T, D])

        v_bank = [bank(f"v_bank{i}") for i in range(2)]
        a_bank = [bank(f"a_bank{i}") for i in range(2)]
        gu_bank = [bank(f"gu_bank{i}") for i in range(2)]
        pv_bank = bank("pv_bank")
        y_bank = bank("y_bank")

        consts_loaded = sem("consts_loaded")
        consts2_loaded = sem("consts2_loaded")
        minus_half_set = sem("minus_half_set")
        rows_padded, v_padded = sem("rows_padded"), sem("v_padded")
        weights_rounded, weights_split = sem("weights_rounded"), sem("weights_split")
        xnT_full_done, xnT_done = sem("xnT_full_done"), sem("xnT_done")
        x_loaded = sem("x_loaded")
        xres_loaded = sem("xres_loaded")
        stats_done = sem("stats_done")
        moments_done = sem("moments_done")
        var_eps_done = sem("var_eps_done")
        rstd_done = sem("rstd_done")
        xn_done = sem("xn_done")
        v_filled, v_free = sem("v_filled"), sem("v_free")
        a_filled, a_free = sem("a_filled"), sem("a_free")
        gu_filled = sem("gu_filled")
        tanh_done = sem("tanh_done")
        act_done = sem("act_done")
        hidden_u_done = sem("hidden_u_done")
        hidden_done = sem("hidden_done")
        down_done = sem("down_done")
        pv_done = sem("pv_done")
        heads_t_done = sem("heads_t_done")
        den_done = sem("den_done")
        partial_done = sem("partial_done")
        stored = sem("stored")
        split_step = sem("split_step")
        parts_done = sem("parts_done")
        parts_stored = sem("parts_stored")
        rows_loaded = sem("rows_loaded")
        ident_bf_done = sem("ident_bf_done")
        neg_max_high_done, neg_max_done = sem("neg_max_high_done"), sem("neg_max_done")
        shift_stored = sem("shift_stored")
        shift_loaded = sem("shift_loaded")
        top_done = sem("top_done")
        top_at_done = sem("top_at_done")
        picks_done = sem("picks_done")
        gap_done = sem("gap_done")
        gap_exp_done = sem("gap_exp_done")
        gap_step = sem("gap_step")
        gates_done = sem("gates_done")
        gates_stored = sem("gates_stored")
        gates_loaded = sem("gates_loaded")

        V, A = Ring(V_ORDER), Ring(A_ORDER)
        STORES = 3
        SHIFTS = SHIFT_ROWS * H // 2 * T
        SPLIT = 4

        def iterations(eng, iteration):
            def one(it):
                iteration(it, it % DEPTH, [s for s in STAGES if has((s,), it)])
            for it in range(FIRST, LOOP_FROM):
                one(it)
            trips = (FULL[1] - LOOP_FROM + 1) // DEPTH
            end = LOOP_FROM + trips * DEPTH
            with eng.Fori(LOOP_FROM, end - DEPTH + 1, DEPTH) as i:
                for j in range(DEPTH):
                    iteration(i + j if j else i, (LOOP_FROM + j) % DEPTH, list(STAGES))
            for it in range(end, LAST + 1):
                one(it)

        def static_before(ring, it):
            return ring.before(it) if isinstance(it, int) else ring.before_full

        assert V.full % 2 == 0 and A.full % 2 == 0

        block = ctx.enter_context(nc.Block())

        @block.tensor
        def _(pe):
            mm = nc.tensor.matmul

            def iteration(it, phase, stages):
                norm, prep, scan, main, tail = (s in stages for s in STAGES)
                bp, bs, bm, bt = (phase + 2) % DEPTH, (phase + 1) % DEPTH, phase, (phase - 1) % DEPTH

                def v_fill(name):
                    n = V.fill(name, it, stages)
                    if due(n - 1):
                        pe.wait_ge(v_free, n - 1)
                    return v_bank[V.bank(name, stages, static_before(V, it))]

                def a_fill(name):
                    n = A.fill(name, it, stages)
                    if due(n - 1):
                        pe.wait_ge(a_free, n - 1)
                    return a_bank[A.bank(name, stages, static_before(A, it))]

                def project(dst, w, x):
                    for n, (i, j) in enumerate(PASSES):
                        last = mm(dst, w[i], x[j], start=(n == 0), stop=(n == len(PASSES) - 1))
                    return last

                def weighted_values(quad, buf):
                    for t in range(T):
                        for j in range(4):
                            h = 4 * quad + j
                            last = mm(pv_bank[HPAD * j:HPAD * (j + 1), quad % 2 * S:quad % 2 * S + S],
                                      values[:, buf, t, h, :], probs[:, h % PB, t, :],
                                      start=(t == 0), stop=(t == T - 1))
                    last.then_inc(pv_done, 1)

                def down(ch, seq):
                    pe.wait_ge(hidden_done, CHUNKS * seq + ch + 1)
                    for t in range(T):
                        last = mm(y_bank[:, t * D:(t + 1) * D], hidden[:, ch, t * P:(t + 1) * P], wd[:, ch, :],
                                  start=(ch == 0 and t == 0), stop=(ch == CHUNKS - 1), skip_group_check=True)
                    last.then_inc(down_done, 1)

                for s in range(H):
                    if main:
                        if s == 0 and is_at(it, 0):
                            pe.wait_ge(shift_loaded, 16 * (2 * it + 1))
                        dst = a_fill(f"e{s}")
                        n = SLOT_ROWS + SHIFT_ROWS
                        for t in range(T):
                            if t == 1 and s == MAX1_SLOT:
                                pe.wait_ge(neg_max_done, 2 * it + 2)
                            if t == 1 and s == DOWN_AFTER and due(it):
                                pe.wait_ge(partial_done, it)
                            if t == 1 and s in QUAD_SLOTS[::2] and due(2 * it + s // 8):
                                pe.wait_ge(heads_t_done, 2 * it + s // 8)
                            if t == 1 and s == H // 2 - 1:
                                pe.wait_ge(shift_loaded, 16 * (2 * it + 2))
                            if t == 1 and s == H - 1 and scan:
                                pe.wait_ge(shift_loaded, 16 * (2 * it + 3))
                            if t == 1 and s == MAX0_SLOT and tail:
                                pe.wait_ge(v_free, V.fill("out1", it, stages) + 1)
                            last = mm(dst[:, t * S:(t + 1) * S], krows[bm][0:n, s, t * P:(t + 1) * P],
                                      qrows[bm][0:n, s, :], start=True, stop=True)
                        last.then_inc(a_filled, 1)
                    if scan:
                        if s == 0 and is_at(it, -1):
                            pe.wait_ge(rows_loaded, 16 * len(SETS) * (it + 2))
                        dst = v_fill(f"s{s}")
                        for t in range(T):
                            if t == 1 and s == MAX1_SLOT:
                                pe.wait_ge(gates_done, it + 2)
                            if t == 1 and s == MAX0_SLOT:
                                pe.wait_ge(neg_max_done, 2 * it + 3)
                            if t == 1 and s == H - 1 and prep:
                                pe.wait_ge(rows_loaded, 16 * len(SETS) * (it + 3))
                            last = mm(dst[:, t * S:(t + 1) * S], qrows[bs][0:SLOT_ROWS, s, t * P:(t + 1) * P],
                                      krows[bs][0:SLOT_ROWS, s, :], start=True, stop=True)
                        last.then_inc(v_filled, 1)
                    if main and s in CHUNK_IN:
                        ch = CHUNK_IN[s]
                        if is_at(it, 0) and s == 0:
                            pe.wait_ge(weights_split, 2)
                        if due(CHUNKS * it + ch - 1):
                            pe.wait_ge(hidden_u_done, CHUNKS * it + ch - 1)
                        for g in range(2):
                            last = project(gu_bank[ch % 2][:, g * S:(g + 1) * S], [w[:, ch, g, :] for w in wgu],
                                           [part[:, bm, :] for part in xnT])
                        last.then_inc(gu_filled, 1)
                    if tail and s - DOWN_AFTER + H in CHUNK_IN:
                        down(CHUNK_IN[s - DOWN_AFTER + H], it - 1)
                    if main and s - DOWN_AFTER in CHUNK_IN:
                        down(CHUNK_IN[s - DOWN_AFTER], it)
                    if tail and s == 1:
                        pe.wait_ge(a_free, A.behind(f"e{H - 1}", it))
                        weighted_values(QUADS - 1, bt)
                    if main and s in QUAD_SLOTS:
                        pe.wait_ge(a_free, A.fill(f"e{s - 2}", it, stages) + 1)
                        weighted_values(s // 4 - 1, bm)

                    if (main or scan) and s == MAX1_SLOT:
                        dst = a_fill("max1_gates")
                        if main:
                            last = mm(dst[0:SHIFTS, S:S + P], neg_max[:, 1, :, :], ident_bf[:, :],
                                      start=True, stop=True)
                        if scan:
                            for t in range(T):
                                last = nc.tensor.transpose(dst[0:GATES, t * P:(t + 1) * P], gates[:, t, :], ident)
                        last.then_inc(a_filled, 1)
                    if prep and s in (ROPE_SLOT, ROPE_SLOT + 1):
                        if s == ROPE_SLOT:
                            pe.wait_ge(xnT_done, it + 3)
                            if is_at(it, -2):
                                pe.wait_ge(weights_split, 1)
                        swapped = s - ROPE_SLOT
                        dst = v_fill(f"rope{swapped}")
                        for m in range(2):
                            last = project(dst[:, m * S:(m + 1) * S], [w[:, 2 * m + swapped, :] for w in wqk],
                                           [part[:, bp, :] for part in xnT])
                        last.then_inc(v_filled, 1)
                    if prep and s == VG_SLOT:
                        dst = a_fill("vg")
                        for t in range(T):
                            last = mm(dst[:, t * VG:(t + 1) * VG], xnT_full[:, t * P:(t + 1) * P], c("wvg"),
                                      start=True, stop=True)
                        last.then_inc(a_filled, 1)
                    if tail and s in (OUT_SLOT, OUT_SLOT + 1):
                        if s == OUT_SLOT:
                            pe.wait_ge(heads_t_done, 2 * it)
                        t = s - OUT_SLOT
                        dst = v_fill(f"out{t}")
                        for quad in range(QUADS):
                            last = nc.tensor.transpose(dst[:, quad * P:(quad + 1) * P],
                                                       heads_t[:, quad, t * P:(t + 1) * P], ident)
                        last.then_inc(v_filled, 1)
                    if (scan or tail) and s == MAX0_SLOT:
                        dst = a_fill("max0_outT")
                        if scan:
                            if is_at(it, -1):
                                pe.wait_ge(ident_bf_done, 1)
                            last = mm(dst[0:SHIFTS, S:S + P], neg_max[:, 0, :, :], ident_bf[:, :],
                                      start=True, stop=True)
                        if tail:
                            if not main:
                                pe.wait_ge(v_free, V.fill("out1", it, stages) + 1)
                            for t in range(T):
                                last = nc.tensor.transpose(dst[:, t * P:(t + 1) * P], heads[:, t, :], ident)
                        last.then_inc(a_filled, 1)
                    if tail and s in (WO_SLOT, WO_SLOT + 1):
                        t = s - WO_SLOT
                        if t == 0:
                            pe.wait_ge(a_free, A.fill("max0_outT", it, stages) + 1)
                        mm(v_fill(f"wo{t}")[:, 0:D], out_t[:, t * P:(t + 1) * P], wo,
                           start=True, stop=True).then_inc(v_filled, 1)

                    if norm and s == H - 1:
                        pe.wait_ge(xn_done, T * (it + 4))
                        if is_at(it, FIRST):
                            pe.wait_ge(consts_loaded, 16)
                        dst = a_fill("xnT")
                        for t in range(T):
                            last = nc.tensor.transpose(dst[:, t * P:(t + 1) * P], xn[:, t, :], ident)
                        last.then_inc(a_filled, 1)

            iterations(pe, iteration)

        @block.scalar
        def _(act_e):
            act_fn = nc.scalar.activation

            def iteration(it, phase, stages):
                norm, prep, scan, main, tail = (s in stages for s in STAGES)
                bp = (phase + 2) % DEPTH

                def filled(name):
                    act_e.wait_ge(a_filled, A.fill(name, it, stages) + 1)
                    return a_bank[A.bank(name, stages, static_before(A, it))]

                def copy_heads(half, seq):
                    act_e.wait_ge(pv_done, QUADS * seq + 2 * (half + 1))
                    act_fn(heads_t[:, 2 * half:2 * half + 2, :],
                           pv_bank[:, :].rearrange("p (q s) -> p q s", q=2), ACT.Copy).then_inc(heads_t_done, 1)

                def copy_shifts(half, src, n):
                    if due(n - 1):
                        act_e.wait_ge(shift_stored, 16 * (n - 1))
                    return act_fn(shift[:, half, :], src[0:SHIFTS, S:S + P], ACT.Copy)

                for s in range(H):
                    if main:
                        src = filled(f"e{s}")
                        if due(QUADS * it + s // 4 - 1):
                            act_e.wait_ge(pv_done, QUADS * it + s // 4 - 1)
                        act_fn(probs[:, s % PB, :, :], src[:, :].rearrange("p (t s) -> p t s", t=T), ACT.Exp,
                               scale=SCALE).then_inc(a_free, 1)
                    if main and s in CHUNK_IN:
                        ch = CHUNK_IN[s]
                        act_e.wait_ge(gu_filled, CHUNKS * it + ch + 1)
                        if due(CHUNKS * it + ch - 1):
                            act_e.wait_ge(act_done, CHUNKS * it + ch - 1)
                        act_fn(tanh[:, ch % 2, :], gu_bank[ch % 2][:, 0:S], ACT.Tanh, scale=0.5)\
                            .then_inc(tanh_done, 1)
                    if tail and s == 1:
                        copy_heads(1, it - 1)
                    if (main or scan) and s == MAX1_SLOT:
                        src = filled("max1_gates")
                        if main:
                            last = copy_shifts(1, src, 2 * it + 1)
                        if scan:
                            if due(it + 1):
                                act_e.wait_ge(gates_stored, 16 * (it + 1))
                            last = act_fn(gates_t[0:GATES, :], src[0:GATES, 0:S], ACT.Copy)
                        last.then_inc(a_free, 1)
                    if prep and s == VG_SLOT:
                        src = filled("vg")[:, 0:T * VG].rearrange("p (t c) -> p t c", t=T)
                        if is_at(it, -2, -1, 0):
                            act_e.wait_ge(v_padded, 2 * (it + 3))
                        for t in range(T):
                            act_fn(values[:, bp, t, :, 0:HD],
                                   src[:, t, 0:D].rearrange("p (h d) -> p h d", d=HD), ACT.Copy)
                        if due(it + 2):
                            act_e.wait_ge(gates_done, it + 2)
                        act_fn(logits[:, :, :], src[:, :, D:D + GATES], ACT.Copy).then_inc(a_free, 1)
                    if main and s == 9:
                        copy_heads(0, it)
                    if prep and s == 7:
                        act_e.wait_ge(gap_done, 2 * (it + 3))
                        act_fn(gap_exp[:, :, :], gap[:, :, :], ACT.Exp).then_inc(gap_exp_done, 1)
                    if (scan or tail) and s == MAX0_SLOT:
                        src = filled("max0_outT")
                        if scan:
                            last = copy_shifts(0, src, 2 * (it + 1))
                        if tail:
                            last = act_fn(out_t[:, :], src[:, 0:S], ACT.Copy)
                        last.then_inc(a_free, 1)

                    if norm and s == H - 1:
                        src = filled("xnT")
                        if due(it + 3):
                            act_e.wait_ge(xnT_done, it + 3)
                        act_fn(xnT_full[:, :], src[:, 0:S], ACT.Copy).then_inc(xnT_full_done, 1)
                        act_fn(xnT[0][:, phase, :], src[:, 0:S], ACT.Copy).then_inc(a_free, 1)

            iterations(act_e, iteration)

        @block.vector
        def _(dve):
            v = nc.vector

            def pad_values(i):
                v.memset(values[:, i, :, :, :], 0.0).then_inc(v_padded, 1)
                dve.wait_ge(v_padded, 2 * i + 1)
                v.memset(values[:, i, :, :, HD:HD + 1], 1.0).then_inc(v_padded, 1)

            def split_weights(first, end):
                high, low = (w[:, first - SPLIT_FROM:end - SPLIT_FROM] for w in weights)
                n = 1 if first == SPLIT_FROM else 2
                v.tensor_copy(high, const[:, first:end]).then_inc(weights_rounded, 1)
                dve.wait_ge(weights_rounded, n)
                v.tensor_tensor(low, const[:, first:end], high.bitcast(F32), ALU.subtract).then_inc(weights_split, 1)

            def iteration(it, phase, stages):
                norm, prep, scan, main, tail = (s in stages for s in STAGES)
                bp, bt = (phase + 2) % DEPTH, (phase - 1) % DEPTH
                sp, sn = it + 2, it + 3

                def filled(name):
                    dve.wait_ge(v_filled, V.fill(name, it, stages) + 1)
                    return v_bank[V.bank(name, stages, static_before(V, it))]

                def negate_maxima(half, n):
                    v.tensor_scalar(neg_max[:, half, 0, :], row_max[:, half, :], -1.0, None, ALU.mult)\
                        .then_inc(neg_max_high_done, 1)
                    dve.wait_ge(neg_max_high_done, n + 1)
                    v.scalar_tensor_tensor(out=neg_max[:, half, 1, :], in0=row_max[:, half, :], scalar=-1.0,
                                           in1=neg_max[:, half, 0, :], op0=ALU.mult, op1=ALU.subtract)\
                        .then_inc(neg_max_done, 1)

                if is_at(it, FIRST):
                    v.memset(minus_half[:, :], -0.5).then_inc(minus_half_set, 1)
                for s in range(H):
                    if main and s - 1 in CHUNK_IN:
                        ch = CHUNK_IN[s - 1]
                        n = CHUNKS * it + ch
                        dve.wait_ge(tanh_done, n + 1)
                        if due(n - 1):
                            dve.wait_ge(hidden_u_done, n - 1)
                        v.scalar_tensor_tensor(out=act[:, ch % 2, :], in0=tanh[:, ch % 2, :], scalar=1.0,
                                               in1=gu_bank[ch % 2][:, 0:S], op0=ALU.add, op1=ALU.mult)\
                            .then_inc(act_done, 1)
                    if prep and s == 5:
                        dve.wait_ge(a_free, A.fill("vg", it, stages) + 1)
                    if prep and s == 6:
                        dve.wait_ge(top_done, T * (sp + 1))
                    if norm and s == 9:
                        dve.wait_ge(stats_done, T * (sn + 1))
                    if scan:
                        src = filled(f"s{s}")
                        at = s % 8 * T
                        v.tensor_reduce(row_max[:, s // 8, at:at + T], src[:, :].rearrange("p (t k) -> p t k", t=T),
                                        AX_X, ALU.max).then_inc(v_free, 1)
                    if main and s - 1 in CHUNK_IN:
                        dve.wait_ge(act_done, n + 1)
                        if due(n - HU + 1):
                            dve.wait_ge(hidden_done, n - HU + 1)
                        v.tensor_tensor(hidden_u[:, ch % HU, :], act[:, ch % 2, :],
                                        gu_bank[ch % 2][:, S:2 * S], ALU.mult).then_inc(hidden_u_done, 1)

                    if main and s == 0:
                        if due(A.behind("max1_gates", it)):
                            dve.wait_ge(a_filled, A.behind("max1_gates", it))
                        dve.wait_ge(v_free, V.behind(f"s{H - 1}", it))
                        negate_maxima(1, 2 * it + 1)
                    if scan and s == 8:
                        if due(A.behind("max0_outT", it)):
                            dve.wait_ge(a_filled, A.behind("max0_outT", it))
                        dve.wait_ge(v_free, V.fill("s7", it, stages) + 1)
                        negate_maxima(0, 2 * (it + 1))
                    if prep and s == ROPE_SLOT:
                        if is_at(it, -2):
                            dve.wait_ge(consts_loaded, 16)
                        src = filled("rope0")[:, :].rearrange("p (m s) -> p m s", m=2)
                        if due(sp):
                            dve.wait_ge(split_step, SPLIT * sp)
                        v.tensor_tensor(rope_c[:, :, :], src, cos.unsqueeze(1).to_broadcast([P, 2, S]),
                                        ALU.mult).then_inc(v_free, 1)
                    if tail and s == 3:
                        dve.wait_ge(down_done, CHUNKS * it)
                        dve.wait_ge(xres_loaded, 16 * it)
                        v.tensor_tensor(partial[:, :, :], y_bank[:, 0:T * D].rearrange("p (t d) -> p t d", t=T),
                                        xres[:, bt, :, :], ALU.add).then_inc(partial_done, 1)
                    if prep and s == ROPE_SLOT + 1:
                        src = filled("rope1")[:, :].rearrange("p (m s) -> p m s", m=2)
                        v.tensor_tensor(rope_s[:, :, :], src, sin.unsqueeze(1).to_broadcast([P, 2, S]),
                                        ALU.mult).then_inc(v_free, 1)
                    if prep and s == 5:
                        for t in range(T):
                            v.max(top[:, t, :], logits[:, t, 0:E]).then_inc(top_done, 1)
                    if prep and s == 6:
                        for t in range(T):
                            v.max_index(top_at[:, t, :], top[:, t, :], logits[:, t, 0:E]).then_inc(top_at_done, 1)
                        v.tensor_tensor(gap[:, :, 0], top[:, :, 1], top[:, :, 0], ALU.subtract).then_inc(gap_done, 1)
                        v.tensor_scalar(gap[:, :, 1], logits[:, :, E], -1.0, None, ALU.mult).then_inc(gap_done, 1)
                    if tail and s in (OUT_SLOT, OUT_SLOT + 1):
                        t = s - OUT_SLOT
                        src = filled(f"out{t}")[:, :].rearrange("p (h r) -> p h r", r=HPAD)
                        v.reciprocal(den_rec[:, t, :], src[:, :, HD]).then_inc(den_done, 1)
                        if t == 0 and due(A.behind("max0_outT", it)):
                            dve.wait_ge(a_filled, A.behind("max0_outT", it))
                        dve.wait_ge(den_done, T * (it - 1) + t + 1)
                        v.tensor_tensor(heads[:, t, :].rearrange("p (h d) -> p h d", d=HD), src[:, :, 0:HD],
                                        den_rec[:, t, :].unsqueeze(2).to_broadcast([P, H, HD]),
                                        ALU.mult).then_inc(v_free, 1)
                    if prep and s == 7:
                        dve.wait_ge(top_at_done, T * (sp + 1))
                        v.tensor_copy(top_atf[:, :, :], top_at[:, :, 0:2]).then_inc(gap_step, 1)
                    if norm and s == 8:
                        dve.wait_ge(x_loaded, 16 * (sn + 1))
                        for t in range(T):
                            v.bn_stats(stats[:, t, :], xin[:, phase, t, :]).then_inc(stats_done, 1)
                    if prep and s == 8:
                        dve.wait_ge(gap_exp_done, sp + 1)
                        v.tensor_scalar(gap_one[:, :, :], gap_exp[:, :, :], 1.0, None, ALU.add).then_inc(gap_step, 1)
                        dve.wait_ge(gap_step, 5 * sp + 2)
                        v.reciprocal(gap_rec[:, :, :], gap_one[:, :, :]).then_inc(gap_step, 1)
                        dve.wait_ge(gap_step, 5 * sp + 3)
                        v.tensor_scalar(first_w[:, :, :], gap_rec[:, :, :], 0.5, None, ALU.mult).then_inc(gap_step, 1)
                    if norm and s == 9:
                        for t in range(T):
                            v.bn_aggr(moments[:, t, :], stats[:, t, :]).then_inc(moments_done, 1)
                    if tail and s in (WO_SLOT, WO_SLOT + 1):
                        t = s - WO_SLOT
                        src = filled(f"wo{t}")
                        if t == 0 and due(it - 1):
                            dve.wait_ge(stored, 16 * (it - 1))
                        v.tensor_tensor(result[:, t, :], src[:, 0:D], partial[:, t, :], ALU.add).then_inc(v_free, 1)
                    if prep and s == 10:
                        dve.wait_ge(gap_step, 5 * sp + 4)
                        v.tensor_tensor(second_w[:, :, :], gap_exp[:, :, 0:1], first_w[:, :, 0:1], ALU.mult)\
                            .then_inc(gap_step, 1)
                        for t in range(T):
                            v.tensor_scalar(pick_a[:, t, :], c("iota"), top_atf[:, t, 0:1], first_w[:, t, 0:1],
                                            ALU.is_equal, ALU.mult).then_inc(picks_done, 1)
                    if prep and s == 11:
                        dve.wait_ge(gap_step, 5 * sp + 5)
                        for t in range(T):
                            v.tensor_scalar(pick_b[:, t, :], c("iota"), top_atf[:, t, 1:2], second_w[:, t, 0:1],
                                            ALU.is_equal, ALU.mult).then_inc(picks_done, 1)
                    if prep and s == 14:
                        if scan:
                            dve.wait_ge(a_filled, A.fill("max1_gates", it, stages) + 1)
                        v.tensor_copy(gates[:, :, E:GATES], first_w[:, :, 1:2]).then_inc(picks_done, 1)
                        dve.wait_ge(picks_done, 5 * (sp + 1))
                        v.tensor_tensor(gates[:, :, 0:E], pick_a[:, :, :], pick_b[:, :, :], ALU.add)\
                            .then_inc(gates_done, 1)
                    if norm and s == 10:
                        dve.wait_ge(moments_done, T * (sn + 1))
                        v.tensor_scalar(var_eps[:, :], moments[:, :, 1], EPS, None, ALU.add).then_inc(var_eps_done, 1)
                    if norm and s == 13:
                        dve.wait_ge(rstd_done, sn + 1)
                        if prep:
                            dve.wait_ge(a_filled, A.behind("xnT", it))
                        for t in range(T):
                            v.tensor_scalar(xn[:, t, :], xin[:, phase, t, :], moments[:, t, 0:1], rstd[:, t:t + 1],
                                            ALU.subtract, ALU.mult).then_inc(xn_done, 1)
                    if s == 14 and is_at(it, -3):
                        dve.wait_ge(consts_loaded, 16)
                        v.tensor_copy(ident_bf[:, :], ident).then_inc(ident_bf_done, 1)
                        split_weights(SPLIT_FROM, COLS["wgu"][0])
                        pad_values(0)
                    if s == 4 and is_at(it, -2):
                        dve.wait_ge(consts2_loaded, 16)
                        split_weights(COLS["wgu"][0], SPLIT_END)
                        pad_values(1)
                    if s == 14 and is_at(it, -1):
                        pad_values(2)

            iterations(dve, iteration)

        @block.gpsimd
        def _(pool):
            g = nc.gpsimd

            def pad_q(i):
                g.memset(qrows[i][:, :, :].bitcast(F32), 0.0).then_inc(rows_padded, 1)

            def pad_k(i):
                g.memset(krows[i][0:SLOT_ROWS, :, :].bitcast(F32), 0.0).then_inc(rows_padded, 1)
                pool.wait_ge(rows_padded, 3 * i + 2)
                g.memset(krows[i][SLOT_ROWS:P, :, :].bitcast(F32), TWO_ONES).then_inc(rows_padded, 1)
                pool.wait_ge(rows_padded, 3 * i + 3)

            def iteration(it, phase, stages):
                norm, prep, scan, main, tail = (s in stages for s in STAGES)
                bp = (phase + 2) % DEPTH
                sp = it + 2
                for s in range(H):
                    if prep and s == 0:
                        pool.wait_ge(xnT_full_done, sp + 1)
                        pool.wait_ge(a_free, A.behind("xnT", it))
                        g.tensor_tensor(xnT[1][:, bp, :], xnT_full[:, :], xnT[0][:, bp, :].bitcast(F32),
                                        ALU.subtract).then_inc(xnT_done, 1)
                    if s == 0 and is_at(it, -3):
                        pad_q(0)
                    if s == 1 and is_at(it, -2):
                        pad_k(0)
                    if s == 1 and is_at(it, -1):
                        pad_q(1)
                        pad_k(1)
                    if s == 15 and is_at(it, -1):
                        pad_q(2)
                        pad_k(2)
                    if scan and s == 6:
                        pool.wait_ge(gates_loaded, 16 * 3 * (it + 2))
                    if main and s - 1 in CHUNK_IN:
                        ch = CHUNK_IN[s - 1]
                        pool.wait_ge(hidden_u_done, CHUNKS * it + ch + 1)
                        if due(CHUNKS * (it - 1) + ch + 1):
                            pool.wait_ge(down_done, CHUNKS * (it - 1) + ch + 1)
                        g.tensor_tensor(hidden[:, ch, :], hidden_u[:, ch % HU, :],
                                        gates_b[phase][:, min(ch, PAIRS), :], ALU.mult).then_inc(hidden_done, 1)
                    if prep and s == 3:
                        pool.wait_ge(v_free, V.fill("rope1", it, stages) + 1)
                        if due(sp):
                            pool.wait_ge(parts_done, sp)
                        g.tensor_tensor(qk[:, :, :], rope_c[:, :, :], rope_s[:, :, :], ALU.add)\
                            .then_inc(split_step, 1)
                        if due(sp):
                            pool.wait_ge(parts_stored, 16 * STORES * sp)
                        g.tensor_tensor(parts[:, PART_AT[0], :], rope_c[:, :, :], rope_s[:, :, :], ALU.add)\
                            .then_inc(split_step, 1)
                    if prep and s == 4:
                        pool.wait_ge(split_step, SPLIT * sp + 2)
                        g.tensor_tensor(parts[:, PART_AT[1], :], qk[:, :, :], parts[:, PART_AT[0], :], ALU.subtract)\
                            .then_inc(split_step, 1)
                    if prep and s == 5:
                        g.tensor_tensor(qk_rest[:, :, :], qk[:, :, :], parts[:, PART_AT[0], :], ALU.subtract)\
                            .then_inc(split_step, 1)
                        pool.wait_ge(split_step, SPLIT * sp + 4)
                        g.tensor_tensor(parts[:, PART_AT[2], :], qk_rest[:, :, :], parts[:, PART_AT[1], :],
                                        ALU.subtract).then_inc(parts_done, 1)
                    if norm and s == 10:
                        if is_at(it, FIRST):
                            pool.wait_ge(minus_half_set, 1)
                        pool.wait_ge(var_eps_done, it + 4)
                        if due(it + 3):
                            pool.wait_ge(xn_done, T * (it + 3))
                        g.tensor_tensor(rstd[:, :], var_eps[:, :], minus_half[:, :], ALU.pow).then_inc(rstd_done, 1)

            iterations(pool, iteration)

        @block.sync
        def _(sp_e):
            dma = sp_e.dma_start

            def rows_of(ap, seq):
                return ap[seq].rearrange("(p t) d -> p t d", t=T)

            def iteration(it, phase, stages):
                norm, prep, scan, main, tail = (s in stages for s in STAGES)
                bp, bs, bm, bt = (phase + 2) % DEPTH, (phase + 1) % DEPTH, phase, (phase - 1) % DEPTH
                seq = it + 2

                def load_shifts(half, n, buf):
                    sp_e.wait_ge(shift_stored, 16 * (n + 1))
                    cols = slice(half * H // 2, (half + 1) * H // 2)
                    dma(qrows[buf][SLOT_ROWS:SLOT_ROWS + SHIFT_ROWS, cols, :].rearrange("r h (t q) -> r (h t) q", t=T),
                        shift_dram[buf, half]).then_inc(shift_loaded, 16)

                if norm:
                    if due(it + 3):
                        sp_e.wait_ge(xn_done, T * (it + 3))
                    dma(xin[:, phase, :, :], rows_of(x, it + 3)).then_inc(x_loaded, 16)
                if is_at(it, FIRST):
                    dma(const[:, 0:SMALL_COLS], consts[:, 0:SMALL_COLS]).then_inc(consts_loaded, 16)
                    dma(const[:, SMALL_COLS:], consts[:, SMALL_COLS:]).then_inc(consts2_loaded, 16)
                if main or scan:
                    sp_e.wait_ge(a_free, A.fill("max1_gates", it, stages) + 1)
                    if main:
                        dma(shift_dram[bm, 1].rearrange("r c q -> (r c) q"), shift[:, 1, :]).then_inc(shift_stored, 16)
                    if scan:
                        dma(gates_dram[bs], gates_t[0:GATES, :]).then_inc(gates_stored, 16)
                if main:
                    load_shifts(1, 2 * it + 1, bm)
                if scan:
                    sp_e.wait_ge(gates_stored, 16 * (it + 2))
                    for half in range(2):
                        dma(gates_b[bs][half * EH:(half + 1) * EH, 0:PAIRS, :],
                            gates_dram[bs, half:E:2, :].partition_broadcast(EH)).then_inc(gates_loaded, 16)
                    dma(gates_b[bs][:, PAIRS, :], gates_dram[bs, E, :].partition_broadcast(P))\
                        .then_inc(gates_loaded, 16)
                if main:
                    if due(it):
                        sp_e.wait_ge(partial_done, it)
                    dma(xres[:, bm, :, :], rows_of(x, it)).then_inc(xres_loaded, 16)
                if prep:
                    def scratch(i, first, count):
                        return parts_dram[bp, i, :, :, first:first + count, :].rearrange("m p j c -> p m j c")

                    sp_e.wait_ge(parts_done, seq + 1)
                    for i, first, count, held in ((0, 0, 3, slice(0, 6)), (1, 0, 2, slice(1, 5)),
                                                  (1, 2, 1, slice(2, 4))):
                        dma(scratch(i, first, count), parts[:, held, :].rearrange("p (m j) c -> p m j c", m=2))\
                            .then_inc(parts_stored, 16)
                    if is_at(it, -2, -1, 0):
                        sp_e.wait_ge(rows_padded, 3 * (seq + 1))
                if scan:
                    sp_e.wait_ge(a_free, A.fill("max0_outT", it, stages) + 1)
                    dma(shift_dram[bs, 0].rearrange("r c q -> (r c) q"), shift[:, 0, :]).then_inc(shift_stored, 16)
                if prep:
                    sp_e.wait_ge(parts_stored, 16 * STORES * (seq + 1))
                    for i in range(len(SETS)):
                        dma(rows[bp][i * SET_ROWS:(i + 1) * SET_ROWS].rearrange("r m h c -> r (m h) c"),
                            parts_dram[bp, i].rearrange("m (h d) j c -> (d j) (m h) c", d=HD))\
                            .then_inc(rows_loaded, 16)
                if scan:
                    load_shifts(0, 2 * (it + 1), bs)
                if tail:
                    sp_e.wait_ge(v_free, V.fill("wo1", it, stages) + 1)
                    dma(rows_of(out, it - 1), result[:, :, :]).then_inc(stored, 16)

            iterations(sp_e, iteration)
            sp_e.wait_ge(stored, 16 * B)


def constants():
    token = (T * np.arange(P)[None, :] + np.arange(T)[:, None]).reshape(S).astype(np.float32)
    inv = (1.0 / 10000.0 ** (np.arange(0, HD, 2, dtype=np.float32) / HD)).astype(np.float32)
    angle = inv[:, None] * token[None, :]
    cos = np.tile(np.repeat(np.cos(angle), 2, axis=0), (H, 1))
    sin = np.tile(np.stack([-np.sin(angle), np.sin(angle)], axis=1).reshape(HD, S), (H, 1))
    return np.eye(P, dtype=np.float32), np.tile(np.arange(E, dtype=np.float32), (P, 1)), \
        cos.astype(np.float32), sin.astype(np.float32)


def kernel(L0_attn_x, L0_attn_wq, L0_attn_wk, L0_attn_wv, L0_attn_wo, L0_ffn_Wg, L0_ffn_We_gate, L0_ffn_We_up,
           L0_ffn_We_down, L0_ffn_Ws_gate, L0_ffn_Ws_up, L0_ffn_Ws_down, L0_ffn_Wsg):
    import concourse.bacc as bacc
    from concourse.bass_utils import run_bass_kernel_spmd

    ident, iota, cos, sin = constants()
    swap = np.arange(D).reshape(D // 2, 2)[:, ::-1].reshape(D)
    a = [np.asarray(w) for w in (L0_attn_wq, L0_attn_wk, L0_attn_wv, L0_attn_wo, L0_ffn_Wg, L0_ffn_Wsg)]
    wq, wk, wv, wo, wg, wsg = a
    eg, eu, ed, sg, su, sd = [np.asarray(w) for w in (L0_ffn_We_gate, L0_ffn_We_up, L0_ffn_We_down,
                                                      L0_ffn_Ws_gate, L0_ffn_Ws_up, L0_ffn_Ws_down)]
    gate = np.concatenate([eg.reshape(E * EH, D), sg]).reshape(CHUNKS, P, D)
    up = np.concatenate([eu.reshape(E * EH, D), su]).reshape(CHUNKS, P, D)
    gate_up = np.stack([gate, up], axis=1).transpose(3, 0, 1, 2).reshape(D, CHUNKS * 2 * P)
    down = np.concatenate([ed.transpose(0, 2, 1).reshape(E * EH, D), sd.T]).reshape(CHUNKS, P, D)
    down = down.transpose(1, 0, 2).reshape(P, CHUNKS * D)
    consts = np.concatenate([ident, iota, cos, sin, wv.T, wg.T, wsg.T, np.zeros((D, VG - D - GATES), wv.dtype),
                             wq.T, wq[swap].T, wk.T, wk[swap].T, gate_up, wo.T, down], axis=1)
    arrays = {"x": np.ascontiguousarray(L0_attn_x), "consts": np.ascontiguousarray(consts)}

    nc = bacc.Bacc("TRN2", target_bir_lowering=False, num_devices=1)
    x_ap = nc.dram_tensor("x", (B, S, D), F32, kind="ExternalInput").ap()
    c_ap = nc.dram_tensor("consts", (P, CONST_COLS), F32, kind="ExternalInput").ap()
    o_ap = nc.dram_tensor("out", (B, S, D), F32, kind="ExternalOutput").ap()
    build(nc, x_ap, c_ap, o_ap)
    r = run_bass_kernel_spmd(nc, [arrays], core_ids=[0])
    return r.results[0]["out"]
```
